# Optimizing a Trainium2 kernel written in Bass

```python
import numpy as np
import jax
import jax.numpy as jnp

def _softmax(x, axis=-1):
    return jax.nn.softmax(x, axis=axis)

def _gelu(x):
    return jax.nn.gelu(x, approximate=True)

def _silu(x):
    return jax.nn.silu(x)

def _sigmoid(x):
    return jax.nn.sigmoid(x)

def _layernorm(x, axis=-1, eps=1e-05):
    m = jnp.mean(x, axis=axis, keepdims=True)
    v = jnp.var(x, axis=axis, keepdims=True)
    return (x - m) / jnp.sqrt(v + eps)

def _scatter_add(tgt, idx, src, axis=0):
    return tgt.at[idx].add(src)

def _segment_sum(src, seg, n):
    return jax.ops.segment_sum(src, seg, n)
kernel_name = 'mk_gps_d2_gnn_r8_6f8a42'

def setup_inputs(seed: int=0):
    np.random.seed(seed)
    _w = jnp.asarray

    def _rec_inputs():
        import jax
        import jax.numpy as jnp
        _gk = jax.random.key(seed)
        x = -8.776e-05 + 1 * jax.random.normal(jax.random.fold_in(_gk, 1), (2500, 256), jnp.float32)
        src = jax.random.randint(jax.random.fold_in(_gk, 2), (80000,), 0, 2500, jnp.int32)
        dst = jnp.minimum((2500 * jax.random.uniform(jax.random.fold_in(_gk, 3), (80000,)) ** 2.0).astype(jnp.int32), 19999)
        _o = jnp.argsort(dst, stable=True)
        src = src[_o]
        dst = dst[_o]
        return (x, src, dst)
    x, src, dst = _rec_inputs()

    def _L0_gnn_setup():
        import jax, jax.numpy as jnp
        import numpy as np
        N_NODES = 2500
        BN_EPS = 1e-05

        def _sage(x, src, dst, W_l, b_l, W_r):
            msg_sum = jax.ops.segment_sum(x[src], dst, num_segments=N_NODES)
            cnt = jax.ops.segment_sum(jnp.ones((src.shape[0],), x.dtype), dst, num_segments=N_NODES)
            aggr = msg_sum / jnp.maximum(cnt, 1.0)[:, None]
            return aggr @ W_l.T + b_l + x @ W_r.T
        key = jax.random.key(seed)
        ks = jax.random.split(key, 8)
        in_dim, half, out_dim, n_edges = (256, 128, 256, 40000)
        s = 1.0 / np.sqrt(in_dim)
        return {'x': jax.random.normal(ks[0], (N_NODES, in_dim), dtype=jnp.float32), 'edge_index': jax.random.randint(ks[1], (2, n_edges), 0, N_NODES, dtype=jnp.int64), 'W_l_f': jax.random.normal(ks[2], (half, in_dim), dtype=jnp.float32) * s, 'b_l_f': jnp.zeros((half,), dtype=jnp.float32), 'W_r_f': jax.random.normal(ks[3], (half, in_dim), dtype=jnp.float32) * s, 'W_l_b': jax.random.normal(ks[4], (half, in_dim), dtype=jnp.float32) * s, 'b_l_b': jnp.zeros((half,), dtype=jnp.float32), 'W_r_b': jax.random.normal(ks[5], (half, in_dim), dtype=jnp.float32) * s, 'gamma': jnp.ones((out_dim,), dtype=jnp.float32), 'beta': jnp.zeros((out_dim,), dtype=jnp.float32)}
    _L0_gnn_all = _L0_gnn_setup()
    _L0_gnn_in = {k: v for k, v in _L0_gnn_all.items() if k in ('W_l_f', 'b_l_f', 'W_r_f', 'W_l_b', 'b_l_b', 'W_r_b', 'gamma', 'beta')}
    del _L0_gnn_all

    def _L0_mix_setup():
        import jax, jax.numpy as jnp
        import numpy as np
        A, Bc, Cc = (0.5, 1.0, 1.0)
        H = 8
        EPS = 1e-12

        def _normalize(t):
            n = jnp.linalg.norm(t, axis=-1, keepdims=True)
            return t / jnp.maximum(n, EPS)
        key = jax.random.key(seed)
        ks = jax.random.split(key, 5)
        B, N, C = (8, 256, 256)
        D = C // H
        x = jax.random.normal(ks[0], (B, N, C), dtype=jnp.float32)
        Wqkv = jax.random.normal(ks[1], (3 * H * D, C), dtype=jnp.float32) * 0.02
        bqkv = jnp.zeros((3 * H * D,), dtype=jnp.float32)
        Wproj = jax.random.normal(ks[2], (C, H * D), dtype=jnp.float32) * 0.02
        bproj = jnp.zeros((C,), dtype=jnp.float32)
        temperature = jnp.ones((1, H, 1, 1), dtype=jnp.float32)
        return {'x': x, 'Wqkv': Wqkv, 'bqkv': bqkv, 'Wproj': Wproj, 'bproj': bproj, 'temperature': temperature}
    _L0_mix_all = _L0_mix_setup()
    _L0_mix_in = {k: v for k, v in _L0_mix_all.items() if k in ('Wqkv', 'bqkv', 'Wproj', 'bproj', 'temperature')}
    del _L0_mix_all

    def _L0_ffn_setup():
        import jax, jax.numpy as jnp
        import numpy as np
        B, S, D, F, E, K = (8, 256, 256, 1024, 8, 2)
        key = jax.random.key(seed)
        ks = jax.random.split(key, 10)
        s = 0.02
        return {'x': jax.random.normal(ks[0], (B, S, D), dtype=jnp.float32), 'Wr': jax.random.normal(ks[1], (D, E), dtype=jnp.float32) * s, 'W1s': jax.random.normal(ks[2], (D, F), dtype=jnp.float32) * s, 'b1s': jnp.zeros((F,), dtype=jnp.float32), 'W2s': jax.random.normal(ks[3], (F, D), dtype=jnp.float32) * s, 'b2s': jnp.zeros((D,), dtype=jnp.float32), 'W1p': jax.random.normal(ks[4], (E, D, F), dtype=jnp.float32) * s, 'b1p': jnp.zeros((E, F), dtype=jnp.float32), 'W2p': jax.random.normal(ks[5], (E, F, D), dtype=jnp.float32) * s, 'b2p': jnp.zeros((E, D), dtype=jnp.float32)}
    _L0_ffn_all = _L0_ffn_setup()
    _L0_ffn_in = {k: v for k, v in _L0_ffn_all.items() if k in ('Wr', 'W1s', 'b1s', 'W2s', 'b2s', 'W1p', 'b1p', 'W2p', 'b2p')}
    del _L0_ffn_all

    def _L1_gnn_setup():
        import jax, jax.numpy as jnp
        import numpy as np
        EPS = 1e-05
        N_NODES = 1250
        N_EDGES = 40000
        D_IN = 256
        D_OUT = 256
        key = jax.random.key(seed)
        k_x, k_e, k_wl, k_bl, k_wr = jax.random.split(key, 5)
        x = jax.random.normal(k_x, (N_NODES, D_IN), dtype=jnp.float32)
        edge_index = jax.random.randint(k_e, (2, N_EDGES), 0, N_NODES, dtype=jnp.int64)
        gamma = jnp.ones((D_IN,), dtype=jnp.float32)
        beta = jnp.zeros((D_IN,), dtype=jnp.float32)
        s = 1.0 / np.sqrt(D_IN)
        W_l = jax.random.uniform(k_wl, (D_OUT, D_IN), dtype=jnp.float32, minval=-s, maxval=s)
        b_l = jax.random.uniform(k_bl, (D_OUT,), dtype=jnp.float32, minval=-s, maxval=s)
        W_r = jax.random.uniform(k_wr, (D_OUT, D_IN), dtype=jnp.float32, minval=-s, maxval=s)
        return {'x': x, 'edge_index': edge_index, 'gamma': gamma, 'beta': beta, 'W_l': W_l, 'b_l': b_l, 'W_r': W_r}
    _L1_gnn_all = _L1_gnn_setup()
    _L1_gnn_in = {k: v for k, v in _L1_gnn_all.items() if k in ('gamma', 'beta', 'W_l', 'b_l', 'W_r')}
    del _L1_gnn_all

    def _L1_mix_setup():
        import jax, jax.numpy as jnp
        import numpy as np
        HEADS, DIM_HEAD = (8, 64)
        EPS = 1e-05

        def instance_norm(t):
            mu = jnp.mean(t, axis=-1, keepdims=True)
            var = jnp.mean((t - mu) ** 2, axis=-1, keepdims=True)
            return (t - mu) * jax.lax.rsqrt(var + EPS)
        key = jax.random.key(seed)
        k1, k2, k3, k4 = jax.random.split(key, 4)
        B, N, D = (8, 1024, 256)
        inner = HEADS * DIM_HEAD
        x = jax.random.normal(k1, (B, N, D), jnp.float32)
        w_qkv = jax.random.normal(k2, (3 * inner, D), jnp.float32) / np.sqrt(D).astype(np.float32)
        w_out = jax.random.normal(k3, (D, inner), jnp.float32) / np.sqrt(inner).astype(np.float32)
        b_out = 0.01 * jax.random.normal(k4, (D,), jnp.float32)
        return {'x': x, 'w_qkv': w_qkv, 'w_out': w_out, 'b_out': b_out}
    _L1_mix_all = _L1_mix_setup()
    _L1_mix_in = {k: v for k, v in _L1_mix_all.items() if k in ('w_qkv', 'w_out', 'b_out')}
    del _L1_mix_all

    def _L1_ffn_setup():
        import jax, jax.numpy as jnp
        import numpy as np
        DIM = 256
        H = 8
        D = 64
        G = 64
        INNER = H * D
        SCALE = D ** (-0.5)
        key = jax.random.key(seed)
        ks = jax.random.split(key, 12)
        B, N = (4, 2048)
        x = jax.random.normal(ks[0], (B, N, DIM), dtype=jnp.float32)
        s = lambda fan_in: 1.0 / np.sqrt(fan_in)
        W_fx = jax.random.normal(ks[1], (DIM, INNER), dtype=jnp.float32) * s(DIM)
        b_fx = jnp.zeros((INNER,), dtype=jnp.float32)
        W_x = jax.random.normal(ks[2], (DIM, INNER), dtype=jnp.float32) * s(DIM)
        b_x = jnp.zeros((INNER,), dtype=jnp.float32)
        A = jax.random.normal(ks[3], (G, D), dtype=jnp.float32)
        Q, _ = jnp.linalg.qr(A.T)
        W_slice = Q[:, :G].astype(jnp.float32)
        b_slice = jnp.zeros((G,), dtype=jnp.float32)
        W_q = jax.random.normal(ks[4], (D, D), dtype=jnp.float32) * s(D)
        W_k = jax.random.normal(ks[5], (D, D), dtype=jnp.float32) * s(D)
        W_v = jax.random.normal(ks[6], (D, D), dtype=jnp.float32) * s(D)
        W_out = jax.random.normal(ks[7], (INNER, DIM), dtype=jnp.float32) * s(INNER)
        b_out = jnp.zeros((DIM,), dtype=jnp.float32)
        temperature = jnp.ones((1, H, 1, 1), dtype=jnp.float32) * 0.5
        return {'x': x, 'W_fx': W_fx, 'b_fx': b_fx, 'W_x': W_x, 'b_x': b_x, 'W_slice': W_slice, 'b_slice': b_slice, 'W_q': W_q, 'W_k': W_k, 'W_v': W_v, 'W_out': W_out, 'b_out': b_out, 'temperature': temperature}
    _L1_ffn_all = _L1_ffn_setup()
    _L1_ffn_in = {k: v for k, v in _L1_ffn_all.items() if k in ('W_fx', 'b_fx', 'W_x', 'b_x', 'W_slice', 'b_slice', 'W_q', 'W_k', 'W_v', 'W_out', 'b_out', 'temperature')}
    del _L1_ffn_all
    return {'x': x, 'src': src, 'dst': dst, 'L0_gnn_W_l_f': _L0_gnn_in['W_l_f'], 'L0_gnn_b_l_f': _L0_gnn_in['b_l_f'], 'L0_gnn_W_r_f': _L0_gnn_in['W_r_f'], 'L0_gnn_W_l_b': _L0_gnn_in['W_l_b'], 'L0_gnn_b_l_b': _L0_gnn_in['b_l_b'], 'L0_gnn_W_r_b': _L0_gnn_in['W_r_b'], 'L0_gnn_gamma': _L0_gnn_in['gamma'], 'L0_gnn_beta': _L0_gnn_in['beta'], 'L0_mix_Wqkv': _L0_mix_in['Wqkv'], 'L0_mix_bqkv': _L0_mix_in['bqkv'], 'L0_mix_Wproj': _L0_mix_in['Wproj'], 'L0_mix_bproj': _L0_mix_in['bproj'], 'L0_mix_temperature': _L0_mix_in['temperature'], 'L0_ffn_Wr': _L0_ffn_in['Wr'], 'L0_ffn_W1s': _L0_ffn_in['W1s'], 'L0_ffn_b1s': _L0_ffn_in['b1s'], 'L0_ffn_W2s': _L0_ffn_in['W2s'], 'L0_ffn_b2s': _L0_ffn_in['b2s'], 'L0_ffn_W1p': _L0_ffn_in['W1p'], 'L0_ffn_b1p': _L0_ffn_in['b1p'], 'L0_ffn_W2p': _L0_ffn_in['W2p'], 'L0_ffn_b2p': _L0_ffn_in['b2p'], 'L1_gnn_gamma': _L1_gnn_in['gamma'], 'L1_gnn_beta': _L1_gnn_in['beta'], 'L1_gnn_W_l': _L1_gnn_in['W_l'], 'L1_gnn_b_l': _L1_gnn_in['b_l'], 'L1_gnn_W_r': _L1_gnn_in['W_r'], 'L1_mix_w_qkv': _L1_mix_in['w_qkv'], 'L1_mix_w_out': _L1_mix_in['w_out'], 'L1_mix_b_out': _L1_mix_in['b_out'], 'L1_ffn_W_fx': _L1_ffn_in['W_fx'], 'L1_ffn_b_fx': _L1_ffn_in['b_fx'], 'L1_ffn_W_x': _L1_ffn_in['W_x'], 'L1_ffn_b_x': _L1_ffn_in['b_x'], 'L1_ffn_W_slice': _L1_ffn_in['W_slice'], 'L1_ffn_b_slice': _L1_ffn_in['b_slice'], 'L1_ffn_W_q': _L1_ffn_in['W_q'], 'L1_ffn_W_k': _L1_ffn_in['W_k'], 'L1_ffn_W_v': _L1_ffn_in['W_v'], 'L1_ffn_W_out': _L1_ffn_in['W_out'], 'L1_ffn_b_out': _L1_ffn_in['b_out'], 'L1_ffn_temperature': _L1_ffn_in['temperature']}

def reference(x, src, dst, L0_gnn_W_l_f, L0_gnn_b_l_f, L0_gnn_W_r_f, L0_gnn_W_l_b, L0_gnn_b_l_b, L0_gnn_W_r_b, L0_gnn_gamma, L0_gnn_beta, L0_mix_Wqkv, L0_mix_bqkv, L0_mix_Wproj, L0_mix_bproj, L0_mix_temperature, L0_ffn_Wr, L0_ffn_W1s, L0_ffn_b1s, L0_ffn_W2s, L0_ffn_b2s, L0_ffn_W1p, L0_ffn_b1p, L0_ffn_W2p, L0_ffn_b2p, L1_gnn_gamma, L1_gnn_beta, L1_gnn_W_l, L1_gnn_b_l, L1_gnn_W_r, L1_mix_w_qkv, L1_mix_w_out, L1_mix_b_out, L1_ffn_W_fx, L1_ffn_b_fx, L1_ffn_W_x, L1_ffn_b_x, L1_ffn_W_slice, L1_ffn_b_slice, L1_ffn_W_q, L1_ffn_W_k, L1_ffn_W_v, L1_ffn_W_out, L1_ffn_b_out, L1_ffn_temperature):
    import jax
    import jax.numpy as jnp

    def _L0_gnn_ref(x, edge_index, W_l_f, b_l_f, W_r_f, W_l_b, b_l_b, W_r_b, gamma, beta):
        import jax, jax.numpy as jnp
        import numpy as np
        N_NODES = 2500
        BN_EPS = 1e-05

        def _sage(x, src, dst, W_l, b_l, W_r):
            msg_sum = jax.ops.segment_sum(x[src], dst, num_segments=N_NODES)
            cnt = jax.ops.segment_sum(jnp.ones((src.shape[0],), x.dtype), dst, num_segments=N_NODES)
            aggr = msg_sum / jnp.maximum(cnt, 1.0)[:, None]
            return aggr @ W_l.T + b_l + x @ W_r.T
        src, dst = (edge_index[0], edge_index[1])
        h_fwd = _sage(x, src, dst, W_l_f, b_l_f, W_r_f)
        h_bwd = _sage(x, dst, src, W_l_b, b_l_b, W_r_b)
        h = jnp.concatenate([h_fwd, h_bwd], axis=-1)
        mean = jnp.mean(h, axis=0)
        var = jnp.mean(jnp.square(h - mean), axis=0)
        h = (h - mean) * jax.lax.rsqrt(var + BN_EPS) * gamma + beta
        return jax.nn.relu(h)

    def _L0_mix_ref(x, Wqkv, bqkv, Wproj, bproj, temperature):
        import jax, jax.numpy as jnp
        import numpy as np
        A, Bc, Cc = (0.5, 1.0, 1.0)
        H = 8
        EPS = 1e-12

        def _normalize(t):
            n = jnp.linalg.norm(t, axis=-1, keepdims=True)
            return t / jnp.maximum(n, EPS)
        B, N, C = x.shape
        D = C // H
        scale = float(D) ** 0.25
        qkv = (x @ Wqkv.T + bqkv).reshape(B, N, 3, H, D)
        qkv = jnp.transpose(qkv, (2, 0, 3, 1, 4))
        q, k, v = (qkv[0], qkv[1], qkv[2])
        q = q * scale
        v1 = jnp.concatenate([jnp.ones((B, H, N, 1), dtype=v.dtype), v], axis=-1)
        qn = _normalize(q) * (scale * temperature)
        kn = _normalize(k) * scale
        vN = v1 / N
        kv_mod = jnp.einsum('bhni,bhnj,bhne->bhije', kn, kn, vN)
        kv = jnp.einsum('bhnd,bhne->bhde', kn, vN)
        vsum = jnp.sum(vN, axis=-2)[:, :, None, :]
        y = A * jnp.einsum('bhni,bhnj,bhije->bhne', qn, qn, kv_mod) + scale ** 2 * Bc * jnp.einsum('bhnd,bhde->bhne', qn, kv) + scale ** 4 * Cc * vsum
        y_norm, y = (y[..., :1], y[..., 1:])
        y = y / y_norm
        out = jnp.transpose(y, (0, 2, 1, 3)).reshape(B, N, H * D)
        return out @ Wproj.T + bproj

    def _L0_ffn_ref(x, Wr, W1s, b1s, W2s, b2s, W1p, b1p, W2p, b2p):
        import jax, jax.numpy as jnp
        import numpy as np
        B, S, D, F, E, K = (8, 256, 256, 1024, 8, 2)
        gelu = lambda t: jax.nn.gelu(t, approximate=False)
        shared = gelu(x @ W1s + b1s) @ W2s + b2s
        rw = jax.nn.softmax(x @ Wr, axis=-1)
        topw, topi = jax.lax.top_k(rw, K)
        topw = topw / jnp.sum(topw, axis=-1, keepdims=True)
        mask = jnp.sum(jax.nn.one_hot(topi, E, dtype=topw.dtype) * topw[..., None], axis=-2)
        h = gelu(jnp.einsum('bsd,edf->bsef', x, W1p) + b1p)
        priv = jnp.einsum('bsef,efd->bsed', h, W2p) + b2p
        routed = jnp.einsum('bsed,bse->bsd', priv, mask)
        return shared + routed

    def _L1_gnn_ref(x, edge_index, gamma, beta, W_l, b_l, W_r):
        import jax, jax.numpy as jnp
        import numpy as np
        EPS = 1e-05
        N_NODES = 1250
        N_EDGES = 40000
        D_IN = 256
        D_OUT = 256
        mu = jnp.mean(x, axis=-1, keepdims=True)
        var = jnp.mean(jnp.square(x - mu), axis=-1, keepdims=True)
        h = (x - mu) * jax.lax.rsqrt(var + EPS) * gamma + beta
        h = jax.nn.relu(h)
        src, dst = (edge_index[0], edge_index[1])
        n = h.shape[0]
        msg = h[src]
        summed = jax.ops.segment_sum(msg, dst, num_segments=n)
        deg = jax.ops.segment_sum(jnp.ones((src.shape[0],), dtype=h.dtype), dst, num_segments=n)
        agg = summed / jnp.maximum(deg, 1.0)[:, None]
        return agg @ W_l.T + b_l + h @ W_r.T

    def _L1_mix_ref(x, w_qkv, w_out, b_out):
        import jax, jax.numpy as jnp
        import numpy as np
        HEADS, DIM_HEAD = (8, 64)
        EPS = 1e-05

        def instance_norm(t):
            mu = jnp.mean(t, axis=-1, keepdims=True)
            var = jnp.mean((t - mu) ** 2, axis=-1, keepdims=True)
            return (t - mu) * jax.lax.rsqrt(var + EPS)
        B, N, _ = x.shape
        H, Dh = (HEADS, DIM_HEAD)
        qkv = jnp.einsum('bnd,ed->bne', x, w_qkv)
        q, k, v = jnp.split(qkv, 3, axis=-1)

        def to_heads(t):
            return t.reshape(B, N, H, Dh).transpose(0, 2, 1, 3)
        q, k, v = (to_heads(q), to_heads(k), to_heads(v))
        k = instance_norm(k)
        v = instance_norm(v)
        dots = jnp.einsum('bhnd,bhne->bhde', k, v)
        out = jnp.einsum('bhnd,bhde->bhne', q, dots) / N
        out = out.transpose(0, 2, 1, 3).reshape(B, N, H * Dh)
        return jnp.einsum('bne,de->bnd', out, w_out) + b_out

    def _L1_ffn_ref(x, W_fx, b_fx, W_x, b_x, W_slice, b_slice, W_q, W_k, W_v, W_out, b_out, temperature):
        import jax, jax.numpy as jnp
        import numpy as np
        DIM = 256
        H = 8
        D = 64
        G = 64
        INNER = H * D
        SCALE = D ** (-0.5)
        B, N, _ = x.shape
        fx_mid = (x @ W_fx + b_fx).reshape(B, N, H, D).transpose(0, 2, 1, 3)
        x_mid = (x @ W_x + b_x).reshape(B, N, H, D).transpose(0, 2, 1, 3)
        temp = jnp.clip(temperature, 0.1, 5.0)
        slice_weights = jax.nn.softmax((x_mid @ W_slice + b_slice) / temp, axis=-1)
        slice_norm = slice_weights.sum(axis=2)
        slice_token = jnp.einsum('bhnc,bhng->bhgc', fx_mid, slice_weights)
        slice_token = slice_token / (slice_norm[..., None] + 1e-05)
        q = slice_token @ W_q
        k = slice_token @ W_k
        v = slice_token @ W_v
        attn = jax.nn.softmax(jnp.einsum('bhgc,bhkc->bhgk', q, k) * SCALE, axis=-1)
        out_slice = jnp.einsum('bhgk,bhkc->bhgc', attn, v)
        out_x = jnp.einsum('bhgc,bhng->bhnc', out_slice, slice_weights)
        out_x = out_x.transpose(0, 2, 1, 3).reshape(B, N, INNER)
        return out_x @ W_out + b_out
    edge_index = jnp.stack([src, dst])
    xn = _layernorm(x, axis=-1)
    x = x + _L0_gnn_ref(xn, edge_index, L0_gnn_W_l_f, L0_gnn_b_l_f, L0_gnn_W_r_f, L0_gnn_W_l_b, L0_gnn_b_l_b, L0_gnn_W_r_b, L0_gnn_gamma, L0_gnn_beta) + _L0_mix_ref(xn[None], L0_mix_Wqkv, L0_mix_bqkv, L0_mix_Wproj, L0_mix_bproj, L0_mix_temperature)[0]
    x = x + _L0_ffn_ref(_layernorm(x, axis=-1)[None], L0_ffn_Wr, L0_ffn_W1s, L0_ffn_b1s, L0_ffn_W2s, L0_ffn_b2s, L0_ffn_W1p, L0_ffn_b1p, L0_ffn_W2p, L0_ffn_b2p)[0]
    xn = _layernorm(x, axis=-1)
    x = x + _L1_gnn_ref(xn, edge_index, L1_gnn_gamma, L1_gnn_beta, L1_gnn_W_l, L1_gnn_b_l, L1_gnn_W_r) + _L1_mix_ref(xn[None], L1_mix_w_qkv, L1_mix_w_out, L1_mix_b_out)[0]
    x = x + _L1_ffn_ref(_layernorm(x, axis=-1)[None], L1_ffn_W_fx, L1_ffn_b_fx, L1_ffn_W_x, L1_ffn_b_x, L1_ffn_W_slice, L1_ffn_b_slice, L1_ffn_W_q, L1_ffn_W_k, L1_ffn_W_v, L1_ffn_W_out, L1_ffn_b_out, L1_ffn_temperature)[0]
    return x

_drawn_inputs = setup_inputs


def setup_inputs(seed=0):
    import zlib

    import numpy as np

    out = dict(_drawn_inputs(seed))
    spreads = {'L0_gnn_b_l_f': (0.0, 0.8),
     'L0_gnn_b_l_b': (0.0, 0.8),
     'L0_gnn_gamma': (1.0, 0.2),
     'L0_gnn_beta': (0.0, 0.1),
     'L0_mix_bqkv': (0.0, 0.1),
     'L0_mix_bproj': (0.0, 0.1),
     'L0_mix_temperature': (1.0, 0.6),
     'L0_ffn_b1s': (0.0, 0.1),
     'L0_ffn_b2s': (0.0, 0.1),
     'L0_ffn_b1p': (0.0, 0.332),
     'L0_ffn_b2p': (0.0, 0.1),
     'L1_gnn_gamma': (1.0, 0.2),
     'L1_gnn_beta': (0.0, 0.1),
     'L1_ffn_b_fx': (0.0, 0.1),
     'L1_ffn_b_x': (0.0, 0.8),
     'L1_ffn_b_slice': (0.0, 0.8),
     'L1_ffn_b_out': (0.0, 0.1),
     'L1_ffn_temperature': (0.5, 0.6)}
    factors = {'L0_mix_Wqkv': 8.0,
     'L1_mix_b_out': 7.77,
     'L1_ffn_W_x': 8.0,
     'L1_ffn_W_slice': 8.0,
     'L1_ffn_W_q': 8.0,
     'L1_ffn_W_k': 8.0}
    for name, (base, spread) in spreads.items():
        noise = np.random.default_rng([zlib.crc32(name.encode()), seed]).standard_normal(out[name].shape)
        drawn = base * np.exp(spread * noise) if base else spread * noise
        out[name] = jnp.asarray(drawn.astype(out[name].dtype))
    for name, factor in factors.items():
        out[name] = (out[name] * factor).astype(out[name].dtype)
    return out
```

```python
import concourse.bass as bass
from concourse import mybir
from contextlib import ExitStack
import numpy as np


class Steps:

    def __init__(self, eng, sem, base=0):
        self.eng, self.sem, self.base, self.n = eng, sem, base, 0

    def then(self, instruction):
        instruction.then_inc(self.sem, 1)
        self.n += 1
        self.eng.wait_ge(self.sem, self.base + self.n)


def graph_network(nc, a, out, stages=99):
    fp32, bf16, fp16, i32 = mybir.dt.float32, mybir.dt.bfloat16, mybir.dt.float16, mybir.dt.int32
    ALU, ACT, AX = mybir.AluOpType, mybir.ActivationFunctionType, mybir.AxisListType
    ds = bass.ds

    N, C = a["x"].shape
    E = a["src"].shape[0]
    P = 128
    T = -(-N // P)
    NP = T * P
    LAST = N - (T - 1) * P
    CB = C // P
    W = 512
    NB = NP // W
    WT = W // P
    CH = E // P
    GRP = 125
    NG = CH // GRP
    MINP = 3
    CHP = CH - 1 + 2 * MINP
    MID = NP // 2
    assert E == CH * P and NG * GRP == CH and NP % W == 0 and C == 256

    top = ExitStack()

    def sb(stack, name, shape, dt=fp32):
        return stack.enter_context(nc.sbuf_tensor(name, shape, dt))

    live = []

    def sem(name):
        live.append(nc.alloc_semaphore(name))
        return live[-1]

    def recycle():
        nc.clear_and_free_semaphores(live)
        nc.all_engine_barrier()
        live.clear()

    def rows(v, n=P):
        return v.rearrange("(o n) -> o n", o=1).partition_broadcast(n) if len(v.shape) == 1 else v.partition_broadcast(n)

    with top:
        X = sb(top, "X", [P, T, C])
        XN = sb(top, "XN", [P, T, C])
        XT = sb(top, "XT", [P, CB, NP])
        ident = sb(top, "ident", [P, P])
        identb = sb(top, "identb", [P, P], bf16)
        onesb = sb(top, "onesb", [P, P], bf16)
        onesf = sb(top, "onesf", [P, P])
        mask = sb(top, "mask", [P, 1])
        lnst = sb(top, "lnst", [P, T, 6])
        lnmv = sb(top, "lnmv", [P, 3, T])
        lnr = sb(top, "lnr", [P, T])
        bank = [top.enter_context(nc.psum_tensor(f"bank{i}", [P, W], fp32)) for i in range(8)]
        A_dram = nc.dram_tensor("A_dram", [T, P, NP], bf16, kind="Internal").ap()
        AT_dram = nc.dram_tensor("AT_dram", [T + 1, P, T, P], bf16, kind="Internal").ap()

        def newton_rsqrt(dve, st, y, v, tmp):
            st.then(dve.tensor_tensor(tmp, y, y, ALU.mult))
            st.then(dve.tensor_tensor(tmp, tmp, v, ALU.mult))
            st.then(dve.tensor_scalar(tmp, tmp, -0.5, 1.5, ALU.mult, ALU.add))
            st.then(dve.tensor_tensor(y, y, tmp, ALU.mult))

        def norm_stage(tag, eps=1e-5, gamma=None, beta=None, split=None, xt=True, first=False):
            source = XN if gamma is not None else X
            s_stat, s_norm, s_tr = sem(tag + "_stats"), sem(tag + "_normed"), sem(tag + "_transposed")
            s_free, s_chain, s_x = sem(tag + "_bank_free"), sem(tag + "_chain"), sem(tag + "_x_loaded")
            s_gp, s_hi, s_mid = sem(tag + "_const"), sem(tag + "_hi"), sem(tag + "_mid")
            s_rest, s_pad, s_gb = sem(tag + "_rest"), sem(tag + "_padded"), sem(tag + "_gb")
            tmp = ExitStack()
            s_var = sem(tag + "_variance")
            s_stg, s_sfree = sem(tag + "_staged"), sem(tag + "_stage_free")
            stg = [sb(tmp, f"{tag}_stage{k}", [P, C]) for k in range(WT)]
            gb = sb(tmp, tag + "_gb", [P, 2, C]) if gamma is not None else None
            with tmp, nc.Block() as block:
                @block.sync
                def _(sp):
                    if first:
                        sp.wait_ge(s_pad, 1)
                        sp.dma_start(X[:, 0:T - 1, :], a["x"][0:(T - 1) * P, :].rearrange("(t p) c -> p t c", p=P)).then_inc(s_x, 16)
                        sp.dma_start(X[0:LAST, T - 1, :], a["x"][(T - 1) * P:N, :]).then_inc(s_x, 16)
                    if gb is not None:
                        sp.dma_start(gb[:, 0, :], rows(gamma)).then_inc(s_gb, 16)
                        sp.dma_start(gb[:, 1, :], rows(beta)).then_inc(s_gb, 16)

                def constants(pool):
                        st = Steps(pool, s_gp)
                        pool.memset(X[:, T - 1, :], 0.0).then_inc(s_pad, 1)
                        pool.memset(onesb[:, :], 1.0)
                        pool.memset(onesf[:, :], 1.0)
                        pool.memset(ident[:, :], 0.0)
                        st.then(pool.memset(mask[:, :], 1.0))
                        st.then(pool.affine_select(out=ident[:, :], in_=ident[:, :], compare_op=ALU.not_equal, fill=1.0,
                                                   base=0, pattern=[[-1, P]], channel_multiplier=1))
                        pool.affine_select(out=mask[:, :], in_=mask[:, :], compare_op=ALU.is_ge, fill=0.0,
                                           base=LAST - 1, pattern=[[0, 1]], channel_multiplier=-1).then_inc(s_gp, 1)
                        pool.tensor_copy(identb[:, :], ident[:, :]).then_inc(s_gp, 1)

                @block.vector
                def _(dve):
                    st = Steps(dve, s_chain)
                    if first:
                        dve.wait_ge(s_x, 32)
                    with dve.Fori(0, T) as t:
                        dve.bn_stats(lnst[:, t, :], source[:, t, :]).then_inc(s_stat, 1)
                    dve.wait_ge(s_stat, T)
                    even, odd = lnst[:, :, 1], lnst[:, :, 4]
                    dve.tensor_tensor(lnmv[:, 0, :], even, odd, ALU.add)
                    dve.tensor_tensor(lnmv[:, 1, :], even, odd, ALU.subtract)
                    st.then(dve.tensor_tensor(lnmv[:, 2, :], lnst[:, :, 2], lnst[:, :, 5], ALU.add))
                    dve.tensor_scalar(lnmv[:, 0, :], lnmv[:, 0, :], 0.5, None, ALU.mult)
                    dve.tensor_scalar(lnmv[:, 2, :], lnmv[:, 2, :], 1.0 / C, None, ALU.mult)
                    st.then(dve.scalar_tensor_tensor(out=lnmv[:, 1, :], in0=lnmv[:, 1, :], scalar=0.25, in1=lnmv[:, 1, :],
                                                     op0=ALU.mult, op1=ALU.mult))
                    dve.scalar_tensor_tensor(out=lnmv[:, 1, :], in0=lnmv[:, 1, :], scalar=eps, in1=lnmv[:, 2, :],
                                             op0=ALU.add, op1=ALU.add).then_inc(s_var, 1)
                    dve.wait_ge(s_var, 2)
                    st.then(dve.reciprocal(lnr[:, :], lnr[:, :]))
                    newton_rsqrt(dve, st, lnr[:, :], lnmv[:, 1, :], lnmv[:, 2, :])
                    if first:
                        dve.wait_ge(s_gp, 4)
                    st.then(dve.tensor_scalar(lnr[:, T - 1:T], lnr[:, T - 1:T], mask[:, 0:1], None, ALU.mult))
                    with dve.Fori(0, T) as t:
                        dve.tensor_scalar(XN[:, t, :], source[:, t, :], lnmv[:, 0, ds(t, 1)], lnr[:, ds(t, 1)],
                                          ALU.subtract, ALU.mult).then_inc(s_norm, 1)
                        if gb is not None:
                            dve.wait_ge(s_gb, 32)
                            dve.wait_ge(s_norm, t * 3 + 1)
                            dve.tensor_tensor(XN[:, t, :], XN[:, t, :], gb[:, 0, :], ALU.mult).then_inc(s_norm, 1)
                            dve.wait_ge(s_norm, t * 3 + 2)
                            dve.tensor_tensor(XN[:, t, :], XN[:, t, :], gb[:, 1, :], ALU.add).then_inc(s_norm, 1)
                    if gb is not None:
                        dve.wait_ge(s_norm, 3 * T)
                        dve.tensor_scalar(XN[:, :, :], XN[:, :, :], 0.0, None, ALU.max).then_inc(s_norm, 1)
                    if split is not None:
                        hi, mid, lo, rest = split
                        dve.wait_ge(s_hi, 1)
                        dve.tensor_tensor(rest[:, :, :], XN[:, :, :], hi[:, :, :], ALU.subtract).then_inc(s_rest, 1)
                        dve.wait_ge(s_mid, 1)
                        dve.tensor_tensor(lo[:, :, :], rest[:, :, :], mid[:, :, :], ALU.subtract).then_inc(s_rest, 1)

                per = 3 if gb is not None else 1

                @block.scalar
                def _(act):
                    act.sem_inc(s_free, CB)
                    act.wait_ge(s_var, 1)
                    act.activation(lnr[:, :], lnmv[:, 1, :], ACT.Sqrt).then_inc(s_var, 1)
                    if split is not None:
                        hi, mid, lo, rest = split
                        act.wait_ge(s_norm, per * T + (gb is not None))
                        act.activation(hi[:, :, :], XN[:, :, :], ACT.Copy).then_inc(s_hi, 1)
                        act.wait_ge(s_rest, 1)
                        act.activation(mid[:, :, :], rest[:, :, :], ACT.Copy).then_inc(s_mid, 1)
                    with act.Fori(0, NB) as b:
                        for h in range(CB):
                            act.wait_ge(s_sfree, b * WT + 2 * WT)
                            act.activation(XT[:, h, ds(b * W, W)], bank[h][:, :], ACT.Copy).then_inc(s_free, 1)

                @block.gpsimd
                def _(pool):
                    if first:
                        constants(pool)
                    pool.sem_inc(s_sfree, WT)
                    with pool.Fori(0, NB) as b:
                        for k in range(WT):
                            if gb is not None:
                                pool.wait_ge(s_norm, 3 * T + 1)
                            else:
                                pool.wait_ge(s_norm, b * WT + (k + 1))
                            pool.wait_ge(s_sfree, b * WT + (k + 1))
                            pool.tensor_copy(stg[k][:, :], XN[:, b * WT + k, :]).then_inc(s_stg, 1)

                @block.tensor
                def _(pe):
                    if first:
                        pe.wait_ge(s_gp, 4)
                    with pe.Fori(0, NB) as b:
                        pe.wait_ge(s_free, b * CB + CB)
                        for k in range(WT):
                            pe.wait_ge(s_stg, b * WT + (k + 1))
                            for h in range(CB):
                                last = pe.transpose(bank[h][:, k * P:(k + 1) * P], stg[k][:, h * P:(h + 1) * P], ident[:, :])
                            last.then_inc(s_sfree, 1)

        def edge_stage():
            tmp = ExitStack()
            s_ld, s_tr, s_ch = sem("edges_loaded"), sem("edges_transposed"), sem("edge_chain")
            s_io, s_par, s_rng = sem("edge_iotas"), sem("ranges_ready"), sem("range_steps")
            s_rdy = [sem("onehot_ready0"), sem("onehot_ready1")]
            s_ohf = [sem("onehot_free0"), sem("onehot_free1")]
            s_bfree = sem("built_bank_free")
            s_tp, s_ate, s_atd, s_ad = sem("tile_transposed"), sem("at_copied"), sem("at_stored"), [sem("a_stored0"), sem("a_stored1")]
            s_zero = sem("strips_zeroed")
            with tmp:
                ei = sb(tmp, "edge_ints", [GRP, 2, NG, P], i32)
                ef = sb(tmp, "edge_floats", [GRP, 2, NG, P])
                ec = sb(tmp, "edge_cols", [P, 2, CHP])
                iot = sb(tmp, "iota_ints", [P, NP], i32)
                ioh = sb(tmp, "iota_half", [P, NP], fp16)
                mm = sb(tmp, "chunk_minmax", [GRP, 2, NG])
                tlo = sb(tmp, "tile_low_i", [GRP, T], i32)
                tlf = sb(tmp, "tile_low", [GRP, 2, T])
                cid = sb(tmp, "chunk_id_i", [GRP, NG], i32)
                cif = sb(tmp, "chunk_id", [GRP, 2, NG])
                hab = sb(tmp, "chunk_reach", [GRP, 2, NG, T])
                val = sb(tmp, "chunk_value", [GRP, 2, T, NG])
                rmx = sb(tmp, "range_max", [GRP, 2, T])
                rcol = sb(tmp, "range_col", [2 * T, 1])
                rrow = sb(tmp, "range_row", [1, 6, T])
                rint = sb(tmp, "range_ints", [1, T], i32)
                par = sb(tmp, "ranges", [1, 3, T], i32)
                ohs = [sb(tmp, f"onehot_src{k}", [P, NP], bf16) for k in range(2)]
                ohd = [sb(tmp, f"onehot_dst{k}", [P, P], bf16) for k in range(2)]
                strip = [sb(tmp, f"a_strip{k}", [P, NP], bf16) for k in range(2)]
                ats = sb(tmp, "at_strip", [P, T, P], bf16)
                tb = [bank[5 + k][:, :].bitcast(bf16).rearrange("p (s d) -> p s d", d=P) for k in range(3)]
                cuts = [(0, 8), (8, 16), (16, T)]

                with nc.Block() as block:
                    @block.sync
                    def _(sp):
                        for k, v in enumerate((a["src"], a["dst"])):
                            sp.dma_start(ei[:, k, :, :], v.rearrange("(g r e) -> r g e", r=GRP, e=P)).then_inc(s_ld, 16)
                        with sp.Fori(0, T // 2) as i:
                            for k in range(2):
                                t = i * 2 + k
                                sp.wait_ge(s_ate, t * 3 + 4)
                                sp.dma_start(AT_dram[t], ats[:, :, :]).then_inc(s_atd, 16)
                                sp.wait_ge(s_bfree, t * 5 + 10)
                                sp.dma_start(A_dram[t], strip[k][:, :]).then_inc(s_ad[k], 16)
                        sp.wait_ge(s_ate, T * 3 + 4)
                        sp.dma_start(AT_dram[T], ats[:, :, :]).then_inc(s_atd, 16)
                        sp.wait_ge(s_atd, 16 * (T + 1))
                        for k in range(2):
                            sp.wait_ge(s_ad[k], 16 * (T // 2))

                    @block.gpsimd
                    def _(pool):
                        pool.iota(iot[:, :], [[1, NP]], base=-MID, channel_multiplier=0).then_inc(s_io, 1)
                        pool.iota(tlo[:, :], [[P, T]], base=0, channel_multiplier=0).then_inc(s_io, 1)
                        pool.iota(cid[:, :], [[GRP, NG]], base=0, channel_multiplier=1).then_inc(s_io, 1)
                        pool.memset(strip[1][:, :], 0.0).then_inc(s_zero, 1)

                    @block.vector
                    def _(dve):
                        st = Steps(dve, s_ch)
                        dve.wait_ge(s_ld, 32)
                        dve.wait_ge(s_io, 3)
                        dve.tensor_copy(ef[:, 1, :, :], ei[:, 1, :, :])
                        dve.tensor_copy(ef[:, 0, :, :], ei[:, 0, :, :])
                        dve.tensor_copy(ioh[:, :], iot[:, :])
                        dve.memset(ec[:, :, CH:CHP], -2.0 * NP)
                        dve.tensor_copy(tlf[:, 0, :], tlo[:, :])
                        dve.tensor_scalar(tlf[:, 1, :], tlo[:, :], float(P - 1), None, ALU.add)
                        dve.tensor_scalar(cif[:, 0, :], cid[:, :], -1.0, float(CH), ALU.mult, ALU.add)
                        dve.tensor_scalar(cif[:, 1, :], cid[:, :], 1.0, None, ALU.add).then_inc(s_rng, 1)
                        dve.wait_ge(s_rng, 1)
                        dve.tensor_reduce(mm[:, 0, :], ef[:, 1, :, :], AX.X, ALU.min)
                        st.then(dve.tensor_reduce(mm[:, 1, :], ef[:, 1, :, :], AX.X, ALU.max))
                        for g in range(NG):
                            dve.tensor_scalar(hab[:, 0, g, :], tlf[:, 1, :], mm[:, 0, g:g + 1], None, ALU.is_ge)
                            st.then(dve.tensor_scalar(hab[:, 1, g, :], tlf[:, 0, :], mm[:, 1, g:g + 1], None, ALU.is_le))
                            for k in range(2):
                                last = dve.scalar_tensor_tensor(out=val[:, k, :, g], in0=hab[:, 0, g, :], scalar=cif[:, k, g:g + 1],
                                                                in1=hab[:, 1, g, :], op0=ALU.mult, op1=ALU.mult)
                            st.then(last)
                        dve.tensor_reduce(rmx[:, :, :], val[:, :, :, :], AX.X, ALU.max).then_inc(s_rng, 1)
                        dve.wait_ge(s_tr, 2 * NG)
                        for k in range(2):
                            for g in range(NG):
                                last = dve.tensor_scalar(ec[:, k, g * GRP:(g + 1) * GRP], bank[2 * k + g // 4][:, (g % 4) * P:(g % 4) * P + GRP],
                                                         -float(MID), None, ALU.add)
                        last.then_inc(s_rng, 1)
                        dve.wait_ge(s_tr, 2 * NG + 1)
                        st.then(dve.tensor_reduce(rcol[:, :], bank[4][0:2 * T, 0:GRP], AX.X, ALU.max))
                        dve.sem_inc(s_rng, 1)
                        dve.wait_ge(s_tr, 2 * NG + 2)
                        src = bank[5][0:1, 0:2 * T]
                        st.then(dve.tensor_copy(rrow[:, 0:2, :], src.rearrange("p (k t) -> p k t", k=2)))
                        st.then(dve.tensor_scalar(rrow[:, 2, :], rrow[:, 0, :], -1.0, float(CH), ALU.mult, ALU.add))
                        st.then(dve.tensor_scalar(rrow[:, 2, :], rrow[:, 2, :], float(CH - 1), None, ALU.min))
                        st.then(dve.scalar_tensor_tensor(out=rint[:, :], in0=rrow[:, 1, :], scalar=1.0, in1=rrow[:, 2, :],
                                                         op0=ALU.add, op1=ALU.subtract))
                        st.then(dve.tensor_scalar(rint[:, :], rint[:, :], 1, None, ALU.arith_shift_right))
                        st.then(dve.tensor_scalar(rrow[:, 3, :], rint[:, :], float(MINP), None, ALU.max))
                        st.then(dve.memset(rrow[:, 5, :], 1.0))
                        st.then(dve.tensor_tensor_scan(rrow[:, 4, :], rrow[:, 5, :], rrow[:, 3, :], 0.0, ALU.mult, ALU.add))
                        st.then(dve.tensor_tensor(rrow[:, 4, :], rrow[:, 4, :], rrow[:, 3, :], ALU.subtract))
                        dve.tensor_copy(par[:, :, :], rrow[:, 2:5, :]).then_inc(s_par, 1)
                        dve.wait_ge(s_par, 1)
                        with dve.Fori(0, T) as t:
                            first = dve.value_load(par[0:1, 0, ds(t, 1)], min_val=0, max_val=CH - 1)
                            pairs = dve.value_load(par[0:1, 1, ds(t, 1)], min_val=MINP, max_val=CH)
                            before = dve.value_load(par[0:1, 2, ds(t, 1)], min_val=0, max_val=CH * T)
                            with dve.Fori(0, pairs) as j:
                                for k in range(2):
                                    dve.wait_ge(s_ohf[k], before + j + 1)
                                    c = nc.s_assert_within(first + j * 2 + k, 0, CHP - 1, skip_runtime_bounds_check_because="a tile ends at most 2 * MINP chunks past its first, or one past its last")
                                    dve.tensor_scalar(ohs[k][:, :], ioh[:, :], ec[:, 0, ds(c, 1)], None, ALU.is_equal)
                                    dve.tensor_scalar(ohd[k][:, :], ioh[:, ds(t * P, P)], ec[:, 1, ds(c, 1)], None, ALU.is_equal)\
                                       .then_inc(s_rdy[k], 1)

                    @block.scalar
                    def _(act):
                        act.sem_inc(s_bfree, 5)
                        act.wait_ge(s_par, 1)
                        act.sem_inc(s_ate, 1)

                        def copy_turned(t):
                            act.wait_ge(s_tp, t + 1)
                            if not isinstance(t, int) or t > 0:
                                act.wait_ge(s_atd, t * 16)
                            for n, (lo, hi) in enumerate(cuts):
                                act.activation(ats[:, lo:hi, :], tb[n][:, 0:hi - lo, :], ACT.Copy).then_inc(s_ate, 1)

                        def pair_of_tiles(i):
                            for k in range(2):
                                t = i * 2 + k
                                copy_turned(t)
                                pairs = act.value_load(par[0:1, 1, ds(t, 1)], min_val=MINP, max_val=CH)
                                before = act.value_load(par[0:1, 2, ds(t, 1)], min_val=0, max_val=CH * T)
                                act.wait_ge(s_ohf[1], before + pairs + 1)
                                if not isinstance(i, int):
                                    act.wait_ge(s_ad[k], i * 16)
                                for b in range(NB):
                                    act.activation(strip[k][:, b * W:(b + 1) * W], bank[b][:, :], ACT.Copy).then_inc(s_bfree, 1)

                        pair_of_tiles(0)
                        with act.Fori(1, T // 2) as i:
                            pair_of_tiles(i)
                        copy_turned(T)

                    @block.tensor
                    def _(pe):
                        pe.wait_ge(s_rng, 1)
                        for k in range(2):
                            for g in range(NG):
                                pe.transpose(bank[2 * k + g // 4][:, (g % 4) * P:(g % 4) * P + GRP], ef[:, k, g, :], ident[0:GRP, 0:GRP]).then_inc(s_tr, 1)
                        pe.wait_ge(s_rng, 2)
                        pe.transpose(bank[4][0:2 * T, 0:GRP], rmx[:, :, :].rearrange("p k t -> p (k t)"), ident[0:GRP, 0:GRP]).then_inc(s_tr, 1)
                        pe.wait_ge(s_rng, 4)
                        pe.transpose(bank[5][0:1, 0:2 * T], rcol[:, :], ident[0:2 * T, 0:2 * T]).then_inc(s_tr, 1)
                        for k in range(2):
                            pe.sem_inc(s_ohf[k], 1)
                        pe.wait_ge(s_par, 1)
                        pe.wait_ge(s_zero, 1)

                        def pair(j, before, start, stop, banks_of=None):
                            for k in range(2):
                                pe.wait_ge(s_rdy[k], before + j + 1)
                                for b in range(NB):
                                    if banks_of is not None and k == 0:
                                        pe.wait_ge(s_bfree, banks_of * 5 + (b + 1))
                                    last = pe.matmul(bank[b][:, :], ohd[k][:, :], ohs[k][:, b * W:(b + 1) * W],
                                                     start=start and k == 0, stop=stop and k == 1)
                                last.then_inc(s_ohf[k], 1)
                            return last

                        def transposes(which, step):
                            pe.wait_ge(s_ate, step * 3 + 1)
                            for s in range(T):
                                n = s // 8
                                last = pe.transpose(tb[n][:, s - 8 * n, :], strip[which][:, s * P:(s + 1) * P], identb[:, :])
                            last.then_inc(s_tp, 1)

                        with pe.Fori(0, T // 2) as i:
                            for k in range(2):
                                t = i * 2 + k
                                pairs = pe.value_load(par[0:1, 1, ds(t, 1)], min_val=MINP, max_val=CH)
                                before = pe.value_load(par[0:1, 2, ds(t, 1)], min_val=0, max_val=CH * T)
                                pair(0, before, True, False, banks_of=t)
                                transposes(1 - k, t)
                                with pe.Fori(1, pairs - 1) as j:
                                    pair(j, before, False, False)
                                pe.wait_ge(s_rdy[0], before + pairs)
                                for b in range(NB):
                                    last = pe.matmul(bank[b][:, :], ohd[0][:, :], ohs[0][:, b * W:(b + 1) * W], start=False, stop=False)
                                last.then_inc(s_ohf[0], 1)
                                pe.wait_ge(s_rdy[1], before + pairs)
                                for b in range(NB - 1):
                                    pe.matmul(bank[b][:, :], ohd[1][:, :], ohs[1][:, b * W:(b + 1) * W], start=False, stop=True)
                                last = pe.matmul(bank[NB - 1][:, :], ohd[1][:, :], ohs[1][:, (NB - 1) * W:], start=False, stop=True)
                                last.then_inc(s_ohf[1], 1)
                        pe.wait_ge(s_bfree, T * 5 + 5)
                        transposes(1, T)

        def spread(ap, axis, n):
            shape = list(ap.shape)
            shape.insert(axis, n)
            return ap.unsqueeze(axis).broadcast_to(shape)

        def split_buffers(stack, tag):
            return [sb(stack, f"{tag}_{part}", [P, T, C], bf16) for part in ("hi", "mid", "lo")]

        def aggregate(tag, stack, split, forward, backward, rest):
            jobs = [(True, b, forward) for b in range(NB)] + ([(False, b, backward) for b in range(NB)] if backward is not None else [])
            s_ld = [sem(f"{tag}_strip_loaded{k}") for k in range(2)]
            s_sum, s_mean, s_ch = sem(tag + "_summed"), sem(tag + "_mean"), sem(tag + "_agg_chain")
            strips = [sb(stack, f"{tag}_strip{k}", [P, T * W], bf16) for k in range(2)]
            recip = sb(stack, tag + "_recip", [P, W])

            def sync(sp):
                for n, (fwd, b, _) in enumerate(jobs):
                    if n >= 2:
                        sp.wait_ge(s_sum, n - 1)
                    if fwd:
                        sp.dma_start(strips[n % 2][:, :].rearrange("p (j x) -> p j x", j=WT),
                                     AT_dram[1 + b * WT:1 + b * WT + WT, :, :, :].rearrange("j p s d -> p j (s d)")).then_inc(s_ld[n % 2], 16)
                    else:
                        sp.dma_start(strips[n % 2][:, :].rearrange("p (t n) -> p t n", t=T),
                                     A_dram[:, :, b * W:(b + 1) * W].rearrange("t p n -> p t n")).then_inc(s_ld[n % 2], 16)

            def tensor(pe):
                for n, (fwd, b, _) in enumerate(jobs):
                    strip = strips[n % 2]
                    pe.wait_ge(s_ld[n % 2], 16 * (n // 2 + 1))
                    if n >= 2:
                        pe.wait_ge(s_mean, n - 1)
                    out3 = bank[3 * (n % 2):3 * (n % 2) + 3]

                    def tile(s, start, stop):
                        if fwd:
                            rhs = strip[:, :].rearrange("p (j s d) -> p j s d", j=WT, s=T)[:, :, s, :]
                        else:
                            rhs = strip[:, :].rearrange("p (t n) -> p t n", t=T)[:, s, :]
                        for h in range(CB):
                            for m, part in enumerate(split):
                                last = pe.matmul(out3[h][:, :], part[:, s, h * P:(h + 1) * P], rhs, start=start and m == 0, stop=stop and m == 2)
                        return pe.matmul(out3[2][:, :], onesb[:, :], rhs, start=start, stop=stop)

                    tile(0, True, False)
                    with pe.Fori(1, T - 1) as s:
                        tile(s, False, False)
                    tile(T - 1, False, True).then_inc(s_sum, 1)

            def vector(dve):
                st = Steps(dve, s_ch)
                for n, (fwd, b, dest) in enumerate(jobs):
                    out3 = bank[3 * (n % 2):3 * (n % 2) + 3]
                    dve.wait_ge(s_sum, n + 1)
                    st.then(dve.tensor_scalar(recip[:, :], out3[2][:, :], 1.0, None, ALU.max))
                    st.then(dve.reciprocal(recip[:, :], recip[:, :]))
                    for h in range(CB):
                        last = dve.tensor_tensor(dest[:, h, b * W:(b + 1) * W], out3[h][:, :], recip[:, :], ALU.mult)
                    last.then_inc(s_mean, 1)
                    dve.wait_ge(s_mean, n + 1)

            return sync, tensor, vector, s_mean, len(jobs)

        def sage_stage(split, rest_split):
            tmp = ExitStack()
            s_w, s_lin, s_h, s_ch = sem("sage_weights"), sem("sage_linear"), sem("sage_h"), sem("sage_chain")
            s_bn, s_relu, s_tr, s_add, s_sq = sem("sage_bn"), sem("sage_relu"), sem("sage_tr"), sem("sage_added"), sem("sage_sqrt")
            with tmp:
                mean = [rest_split, sb(tmp, "mean_b", [P, CB, NP])]
                H = XN[:, :, :].rearrange("p t c -> p (t c)").rearrange("p (d n) -> p d n", d=2)
                wl = sb(tmp, "wl", [P, 2, CB, P])
                wr = sb(tmp, "wr", [P, 2, CB, P])
                vec = sb(tmp, "sage_vec", [P, 3, 2])
                bst = sb(tmp, "bn_stats", [P, 2, NB, 6])
                bmv = sb(tmp, "bn_mv", [P, 2, 2])
                aff = sb(tmp, "bn_affine", [P, 6, 2])
                rel = [sb(tmp, f"relu{k}", [P, 2, W]) for k in range(2)]
                sync, tensor, vector, s_mean, njobs = aggregate("agg0", tmp, split, mean[0], mean[1], None)
                with nc.Block() as block:
                    @block.sync
                    def _(sp):
                        for d, x in enumerate("fb"):
                            sp.dma_start(wl[:, d, :, :], a[f"L0_gnn_W_l_{x}"].rearrange("(k p) o -> p k o", p=P)).then_inc(s_w, 16)
                            sp.dma_start(wr[:, d, :, :], a[f"L0_gnn_W_r_{x}"].rearrange("(k p) o -> p k o", p=P)).then_inc(s_w, 16)
                            sp.dma_start(vec[:, 0, d:d + 1], a[f"L0_gnn_b_l_{x}"].rearrange("(p o) -> p o", o=1)).then_inc(s_w, 16)
                        for n, v in ((1, "gamma"), (2, "beta")):
                            for d in range(2):
                                sp.dma_start(vec[:, n, d:d + 1], a[f"L0_gnn_{v}"][d * P:(d + 1) * P].rearrange("(p o) -> p o", o=1)).then_inc(s_w, 16)
                        sync(sp)

                    @block.tensor
                    def _(pe):
                        tensor(pe)
                        pe.wait_ge(s_w, 160)
                        pe.wait_ge(s_mean, njobs)
                        for n in range(2 * NB):
                            d, b = n // NB, n % NB
                            if n >= 2:
                                pe.wait_ge(s_h, n - 1)
                            cols = slice(b * W, (b + 1) * W)
                            for k in range(CB):
                                pe.matmul(bank[6 + n % 2][:, :], wl[:, d, k, :], mean[d][:, k, cols], start=k == 0, stop=False)
                            for k in range(CB):
                                last = pe.matmul(bank[6 + n % 2][:, :], wr[:, d, k, :], XT[:, k, cols], start=False, stop=k == CB - 1)
                            last.then_inc(s_lin, 1)
                        for b in range(NB):
                            pe.wait_ge(s_relu, 2 * b + 2)
                            if b >= 1:
                                pe.wait_ge(s_add, b)
                            for j in range(WT):
                                for d in range(2):
                                    last = pe.transpose(bank[j // 2][:, (j % 2) * C + d * P:(j % 2) * C + (d + 1) * P],
                                                        rel[b % 2][:, d, j * P:(j + 1) * P], ident[:, :])
                            last.then_inc(s_tr, 1)

                    @block.scalar
                    def _(act):
                        for n in range(2 * NB):
                            d, b = n // NB, n % NB
                            act.wait_ge(s_lin, n + 1)
                            act.activation(H[:, d, b * W:(b + 1) * W], bank[6 + n % 2][:, :], ACT.Identity, bias=vec[:, 0, d:d + 1]).then_inc(s_h, 1)
                        act.wait_ge(s_bn, 1)
                        act.activation(aff[:, 0, :], aff[:, 1, :], ACT.Sqrt).then_inc(s_sq, 1)
                        act.wait_ge(s_bn, 2)
                        for b in range(NB):
                            if b >= 2:
                                act.wait_ge(s_tr, b - 1)
                            for d in range(2):
                                act.activation(rel[b % 2][:, d, :], H[:, d, b * W:(b + 1) * W], ACT.Relu,
                                               bias=aff[:, 4, d:d + 1], scale=aff[:, 3, d:d + 1]).then_inc(s_relu, 1)

                    @block.vector
                    def _(dve):
                        vector(dve)
                        st = Steps(dve, s_ch)
                        for n in range(2 * NB):
                            d, b = n // NB, n % NB
                            dve.wait_ge(s_h, n + 1)
                            st.then(dve.bn_stats(bst[:, d, b, :], H[:, d, b * W:min((b + 1) * W, N)]))
                        for d in range(2):
                            st.then(dve.bn_aggr(bmv[:, d, :], bst[:, d, :, :].rearrange("p b s -> p (b s)")))
                        dve.tensor_scalar(aff[:, 1, :], bmv[:, :, 1], 1e-5, None, ALU.add).then_inc(s_bn, 1)
                        dve.wait_ge(s_sq, 1)
                        st.then(dve.reciprocal(aff[:, 0, :], aff[:, 0, :]))
                        newton_rsqrt(dve, st, aff[:, 0, :], aff[:, 1, :], aff[:, 2, :])
                        st.then(dve.tensor_tensor(aff[:, 3, :], aff[:, 0, :], vec[:, 1, :], ALU.mult))
                        st.then(dve.tensor_tensor(aff[:, 5, :], bmv[:, :, 0], aff[:, 3, :], ALU.mult))
                        dve.tensor_tensor(aff[:, 4, :], vec[:, 2, :], aff[:, 5, :], ALU.subtract).then_inc(s_bn, 1)
                        for b in range(NB):
                            dve.wait_ge(s_tr, b + 1)
                            for k in range(2):
                                last = dve.tensor_tensor(X[:, b * WT + 2 * k:b * WT + 2 * k + 2, :].rearrange("p t c -> p (t c)"),
                                                         X[:, b * WT + 2 * k:b * WT + 2 * k + 2, :].rearrange("p t c -> p (t c)"),
                                                         bank[k][:, :], ALU.add)
                            last.then_inc(s_add, 1)

        def project_stage(tag, sources, loads, bias, out_dram=None, before=None):
            nk = sum(len(w) for _, w in sources)
            tmp = ExitStack()
            s_w, s_stg, s_free = sem(tag + "_w"), sem(tag + "_staged"), sem(tag + "_stage_free")
            s_mm, s_add, s_out = sem(tag + "_product"), sem(tag + "_added"), sem(tag + "_stored")
            with tmp:
                stg = [sb(tmp, f"{tag}_cols{k}", [P, nk, P]) for k in range(2)]
                bb = sb(tmp, tag + "_bias", [P, C])
                with nc.Block() as block:
                    @block.sync
                    def _(sp):
                        sp.dma_start(bb[:, :], rows(bias)).then_inc(s_w, 16)
                        for dst, src in loads:
                            sp.dma_start(dst, src).then_inc(s_w, 16)
                        if out_dram is not None:
                            full = T - 1
                            with sp.Fori(0, full) as t:
                                sp.wait_ge(s_add, t + 1)
                                sp.dma_start(out_dram[ds(t * P, P), :], X[:, t, :]).then_inc(s_out, 16)
                            sp.wait_ge(s_add, T)
                            sp.dma_start(out_dram[full * P:N, :], X[0:LAST, full, :]).then_inc(s_out, 16)
                            sp.wait_ge(s_out, 16 * T)

                    @block.gpsimd
                    def _(pool):
                        pool.wait_ge(s_w, 16 * (1 + len(loads)))
                        pool.sem_inc(s_free, 2)
                        with pool.Fori(0, T // 2) as i:
                            for k in range(2):
                                t = i * 2 + k
                                pool.wait_ge(s_free, t + 1)
                                m = 0
                                for src, w in sources:
                                    pool.tensor_copy(stg[k][:, m:m + len(w), :], src[:, :, ds(t * P, P)])
                                    m += len(w)
                                pool.tensor_tensor(X[:, t, :], X[:, t, :], bb[:, :], ALU.add).then_inc(s_stg, 1)

                    @block.tensor
                    def _(pe):
                        with pe.Fori(0, T // 2) as i:
                            for k in range(2):
                                t = i * 2 + k
                                pe.wait_ge(s_stg, t + 1)
                                m = 0
                                for _, ws in sources:
                                    for w in ws:
                                        last = pe.matmul(bank[k][:, 0:C], stg[k][:, m, :], w, start=m == 0, stop=m == nk - 1)
                                        m += 1
                                last.then_inc(s_mm, 1)

                    @block.vector
                    def _(dve):
                        with dve.Fori(0, T // 2) as i:
                            for k in range(2):
                                t = i * 2 + k
                                dve.wait_ge(s_mm, t + 1)
                                dve.tensor_tensor(X[:, t, :], X[:, t, :], bank[k][:, 0:C], ALU.add).then_inc(s_add, 1)
                                dve.wait_ge(s_add, t + 1)
                                dve.sem_inc(s_free, 1)

        def taylor_stage():
            Hh, D = 8, C // 8
            D1 = D + 1
            JC = D1 // 3
            scale = float(D) ** 0.25
            DH = 5
            tmp = ExitStack()
            s_w, s_stg, s_sfree, s_kv, s_ev = sem("ty_w"), sem("ty_staged"), sem("ty_stage_free"), sem("ty_kv"), sem("ty_evac")
            s_ss, s_sq, s_rt, s_ch = sem("ty_ss"), sem("ty_square"), sem("ty_root"), sem("ty_chain")
            s_kn, s_pd, s_pp, s_pf, s_va = sem("ty_kn"), sem("ty_prod_dve"), sem("ty_prod_pool"), sem("ty_prod_free"), sem("ty_vsum")
            s_m, s_vs, s_qs, s_qt, s_qc = sem("ty_m"), sem("ty_vs"), sem("ty_q_staged"), sem("ty_q_turned"), sem("ty_q_copied")
            s_t, s_tf, s_o, s_ot, s_oc = sem("ty_t"), sem("ty_t_free"), sem("ty_o"), sem("ty_o_turned"), sem("ty_o_copied")
            s_pr, s_add, s_ch2 = sem("ty_projected"), sem("ty_added"), sem("ty_chain2")
            with tmp:
                wt = sb(tmp, "wqkv", [P, CB, 3 * C])
                wp = sb(tmp, "wproj", [P, CB, C])
                bq = sb(tmp, "bqkv", [P, 3 * C])
                bp = sb(tmp, "bproj", [P, C])
                tp = sb(tmp, "ty_factor", [P, 2, Hh])
                stg = [sb(tmp, f"ty_cols{k}", [P, CB, P]) for k in range(2)]
                raw = [sb(tmp, f"ty_raw{k}", [P, 2 * C]) for k in range(2)]
                sq = [sb(tmp, f"ty_sq{k}", [P, 2 * C]) for k in range(2)]
                ss = [sb(tmp, f"ty_ss{k}", [P, 3, 2 * Hh]) for k in range(2)]
                KN = [sb(tmp, f"kn{k}", [P, Hh, D1]) for k in range(2)]
                V1 = [sb(tmp, f"v1{k}", [P, Hh, D1]) for k in range(2)]
                PR = [sb(tmp, f"prod{h}", [P, D1, D1]) for h in range(Hh)]
                M = [sb(tmp, f"m{g}", [P, D1, D1]) for g in range(2)]
                QA = sb(tmp, "q_all", [P, T, Hh, D1])
                vacc = sb(tmp, "vacc", [P, Hh, D1])
                vs = sb(tmp, "vs", [P, Hh, D1])
                zero = sb(tmp, "ty_zero", [P, P])
                Y = sb(tmp, "ty_y", [P, Hh, D1])
                ry = sb(tmp, "ty_ry", [P, Hh])
                QS = [sb(tmp, f"ty_qs{k}", [P, Hh, D]) for k in range(2)]
                O = [sb(tmp, f"ty_o{k}", [P, Hh, D]) for k in range(2)]
                QT = [sb(tmp, f"ty_qt{k}", [P, CB, P]) for k in range(2)]
                OT = [sb(tmp, f"ty_ot{k}", [P, CB, P]) for k in range(2)]

                def by_head(ap):
                    return ap.rearrange("p (h d) -> p h d", d=D)

                with nc.Block() as block:
                    @block.sync
                    def _(sp):
                        sp.dma_start(wt[:, :, :], a["L0_mix_Wqkv"].rearrange("(k p) o -> p k o", p=P)).then_inc(s_w, 16)
                        sp.dma_start(wp[:, :, :], a["L0_mix_Wproj"].rearrange("(k p) o -> p k o", p=P)).then_inc(s_w, 16)
                        sp.dma_start(bq[:, :], rows(a["L0_mix_bqkv"])).then_inc(s_w, 16)
                        sp.dma_start(bp[:, :], rows(a["L0_mix_bproj"])).then_inc(s_w, 16)
                        sp.dma_start(tp[:, 0, :], rows(a["L0_mix_temperature"].rearrange("a h b c -> (a h b c)"))).then_inc(s_w, 16)

                    @block.gpsimd
                    def _(pool):
                        pool.memset(zero[:, :], 0.0)
                        pool.memset(QA[:, :, :, D:D1], 1.0)
                        for k in range(2):
                            pool.memset(KN[k][:, :, D:D1], 1.0)
                            pool.memset(V1[k][:, :, 0:1], 1.0)
                        pool.memset(vacc[:, :, :], 0.0).then_inc(s_va, 1)
                        pool.sem_inc(s_sfree, 2)
                        pool.wait_ge(s_va, 1)
                        with pool.Fori(0, T // 2) as i:
                            for k in range(2):
                                t = i * 2 + k
                                pool.wait_ge(s_sfree, t + 1)
                                pool.tensor_copy(stg[k][:, :, :], XT[:, :, ds(t * P, P)]).then_inc(s_stg, 1)
                                pool.wait_ge(s_kn, t + 1)
                                pool.tensor_tensor(vacc[:, :, :], vacc[:, :, :], V1[k][:, :, :], ALU.add).then_inc(s_va, 1)
                                for h in range(DH, Hh):
                                    pool.wait_ge(s_pf, t * Hh + (h + 2))
                                    pool.tensor_tensor(PR[h][:, :, :], spread(KN[k][:, h, :], 2, D1), spread(V1[k][:, h, :], 1, D1),
                                                       ALU.mult).then_inc(s_pp, 1)
                                pool.wait_ge(s_va, t + 2)

                    @block.tensor
                    def _(pe):
                        pe.wait_ge(s_w, 80)
                        pe.wait_ge(s_va, 1)
                        for g in range(2):
                            for c in range(3):
                                pe.matmul(bank[2 + 3 * g + c][:, 0:JC * D1], zero[:, :], wt[:, 0, 0:JC * D1], start=True, stop=False)
                        pe.sem_inc(s_pf, Hh + 1)

                        def qkv(t, k):
                            pe.wait_ge(s_stg, t + 1)
                            pe.wait_ge(s_sfree, t + 2)
                            for c in range(CB):
                                pe.matmul(bank[0][:, :], stg[k][:, c, :], wt[:, c, 0:2 * C], start=c == 0, stop=c == CB - 1)
                            for c in range(CB):
                                last = pe.matmul(bank[1][:, 0:C], stg[k][:, c, :], wt[:, c, 2 * C:3 * C], start=c == 0, stop=c == CB - 1)
                            last.then_inc(s_kv, 1)

                        def sums(t, k):
                            for h in range(Hh):
                                if h < DH:
                                    pe.wait_ge(s_pd, t * DH + (h + 1))
                                else:
                                    pe.wait_ge(s_pp, t * (Hh - DH) + (h - DH + 1))
                                g, q = h // 4, h % 4
                                flat = PR[h][:, :, :].rearrange("p j e -> p (j e)")
                                for c in range(3):
                                    last = pe.matmul(bank[2 + 3 * g + c][32 * q:32 * q + 32, 0:JC * D1], KN[k][:, h, 0:D],
                                                     flat[:, c * JC * D1:(c + 1) * JC * D1], start=False, stop=False,
                                                     tile_position=(0, 32 * q), skip_group_check=True)
                                last.then_inc(s_pf, 1)

                        qkv(0, 0)
                        with pe.Fori(0, T // 2 - 1) as i:
                            for k in range(2):
                                qkv(i * 2 + (k + 1), 1 - k)
                                sums(i * 2 + k, k)
                        qkv(T - 1, 1)
                        sums(T - 2, 0)
                        sums(T - 1, 1)
                        for n in range(2, 8):
                            last = pe.matmul(bank[n][:, 0:JC * D1], zero[:, :], wt[:, 0, 0:JC * D1], start=False, stop=True)

                    @block.scalar
                    def _(act):
                        with act.Fori(0, T // 2) as i:
                            for k in range(2):
                                t = i * 2 + k
                                act.wait_ge(s_ev, t + 1)
                                act.activation(sq[k][:, :], raw[k][:, :], ACT.Square).then_inc(s_sq, 1)
                                act.wait_ge(s_ss, t + 1)
                                act.activation(ss[k][:, 0, :], ss[k][:, 1, :], ACT.Sqrt).then_inc(s_rt, 1)

                    @block.vector
                    def _(dve):
                        dve.wait_ge(s_w, 80)
                        dve.wait_ge(s_va, 1)
                        st = Steps(dve, s_ch)
                        dve.memset(tp[:, 1, :], scale)
                        st.then(dve.tensor_scalar(tp[:, 0, :], tp[:, 0, :], scale, None, ALU.mult))
                        L = 9

                        def tile(t, k, valid=P):
                            st = Steps(dve, s_ch, base=t * L + 1)
                            dve.wait_ge(s_kv, t + 1)
                            dve.wait_ge(s_pf, t * Hh + 1)
                            dve.tensor_tensor(raw[k][:, :], bank[0][:, :], bq[:, 0:2 * C], ALU.add).then_inc(s_ev, 1)
                            st.then(dve.tensor_tensor(V1[k][:, :, 1:D1], by_head(bank[1][:, 0:C]), by_head(bq[:, 2 * C:3 * C]), ALU.add))
                            dve.sem_inc(s_sfree, 1)
                            if valid < P:
                                st.then(dve.tensor_scalar(V1[k][:, :, :], V1[k][:, :, :], mask[:, 0:1], None, ALU.mult))
                            dve.wait_ge(s_sq, t + 1)
                            st.then(dve.tensor_reduce(ss[k][:, 2, :], by_head(sq[k][:, :]), AX.X, ALU.add))
                            st.then(dve.tensor_scalar(ss[k][:, 2, 0:Hh], ss[k][:, 2, 0:Hh], scale * scale, None, ALU.mult))
                            dve.tensor_scalar(ss[k][:, 1, :], ss[k][:, 2, :], 1e-24, None, ALU.max).then_inc(s_ss, 1)
                            dve.wait_ge(s_rt, t + 1)
                            st.then(dve.reciprocal(ss[k][:, 0, :], ss[k][:, 0, :]))
                            newton_rsqrt(dve, st, ss[k][:, 0, :], ss[k][:, 1, :], ss[k][:, 2, :])
                            st.then(dve.tensor_tensor(ss[k][:, 0, :], ss[k][:, 0, :], tp[:, :, :].rearrange("p a h -> p (a h)"), ALU.mult))
                            assert st.n == L + (valid < P)
                            dve.tensor_tensor(KN[k][:, :, 0:D], by_head(raw[k][:, C:2 * C]), spread(ss[k][:, 0, Hh:2 * Hh], 2, D), ALU.mult)\
                               .then_inc(s_kn, 1)
                            dve.wait_ge(s_kn, t + 1)
                            for h in range(DH):
                                dve.wait_ge(s_pf, t * Hh + (h + 2))
                                dve.tensor_tensor(PR[h][:, :, :], spread(KN[k][:, h, :], 2, D1), spread(V1[k][:, h, :], 1, D1),
                                                  ALU.mult).then_inc(s_pd, 1)
                            dve.scalar_tensor_tensor(out=QA[:, t, :, 0:D], in0=by_head(raw[k][:, 0:C]), scalar=scale,
                                                     in1=spread(ss[k][:, 0, 0:Hh], 2, D), op0=ALU.mult, op1=ALU.mult)

                        with dve.Fori(0, T // 2 - 1) as i:
                            for k in range(2):
                                tile(i * 2 + k, k)
                        tile(T - 2, 0)
                        tile(T - 1, 1, valid=LAST)

                with nc.Block() as block:
                    @block.gpsimd
                    def _(pool):
                        with pool.Fori(0, T // 2) as i:
                            for k in range(2):
                                t = i * 2 + k
                                if k == 0:
                                    pool.wait_ge(s_t, i * (2 * Hh) + 1)
                                pool.tensor_copy(QS[k][:, :, :], QA[:, t, :, 0:D])
                                pool.tensor_tensor(X[:, t, :], X[:, t, :], bp[:, :], ALU.add).then_inc(s_qs, 1)

                    @block.tensor
                    def _(pe):
                        pe.matmul(bank[0][:, 0:Hh * D1], onesf[:, :], vacc[:, :, :].rearrange("p h e -> p (h e)"), start=True, stop=True)\
                          .then_inc(s_vs, 1)
                        pe.wait_ge(s_m, 8)
                        pe.wait_ge(s_vs, 2)
                        pe.sem_inc(s_tf, 2)
                        pe.sem_inc(s_t, 1)

                        def turn(k, source):
                            for c in range(CB):
                                last = pe.transpose(bank[k][:, C + c * P:C + (c + 1) * P],
                                                    source[:, 4 * c:4 * c + 4, :].rearrange("p h d -> p (h d)"), ident[:, :])
                            return last

                        with pe.Fori(0, T // 2) as i:
                            for k in range(2):
                                t = i * 2 + k
                                pe.wait_ge(s_qs, t + 1)
                                turn(k, QS[k]).then_inc(s_qt, 1)
                                pe.wait_ge(s_qc, t + 1)
                                for h in range(Hh):
                                    g, q = h // 4, h % 4
                                    pe.wait_ge(s_tf, t * Hh + (h + 1))
                                    flat = M[g][:, :, :].rearrange("p j e -> p (j e)")
                                    for c in range(3):
                                        last = pe.matmul(bank[2 + 3 * (h % 2) + c][:, 0:JC * D1], QT[k][32 * q:32 * q + 32, g, :],
                                                         flat[32 * q:32 * q + 32, c * JC * D1:(c + 1) * JC * D1], start=True, stop=True,
                                                         tile_position=(32 * q, 0))
                                    last.then_inc(s_t, 1)
                                pe.wait_ge(s_o, t + 1)
                                turn(k, O[k]).then_inc(s_ot, 1)
                                pe.wait_ge(s_oc, t + 1)
                                for c in range(CB):
                                    last = pe.matmul(bank[k][:, 0:C], OT[k][:, c, :], wp[:, c, :], start=c == 0, stop=c == CB - 1)
                                last.then_inc(s_pr, 1)

                    @block.scalar
                    def _(act):
                        for g in range(2):
                            for c in range(3):
                                cols = bank[2 + 3 * g + c][:, 0:JC * D1].rearrange("p (j e) -> p j e", e=D1)
                                n = JC - (c == 2)
                                act.activation(M[g][:, c * JC:c * JC + n, :], cols[:, 0:n, :], ACT.Copy, scale=0.5 / N).then_inc(s_m, 1)
                            act.activation(M[g][:, D:D1, :], cols[:, JC - 1:JC, :], ACT.Copy, scale=scale * scale / N).then_inc(s_m, 1)
                        with act.Fori(0, T // 2) as i:
                            for k in range(2):
                                t = i * 2 + k
                                act.wait_ge(s_qt, t + 1)
                                act.activation(QT[k][:, :, :], bank[k][:, C:2 * C].rearrange("p (c n) -> p c n", c=CB), ACT.Copy).then_inc(s_qc, 1)
                                act.wait_ge(s_ot, t + 1)
                                act.activation(OT[k][:, :, :], bank[k][:, C:2 * C].rearrange("p (c n) -> p c n", c=CB), ACT.Copy).then_inc(s_oc, 1)

                    @block.vector
                    def _(dve):
                        dve.wait_ge(s_vs, 1)
                        dve.tensor_scalar(vs[:, :, :], bank[0][:, 0:Hh * D1].rearrange("p (h e) -> p h e", h=Hh), scale ** 4 / N, None, ALU.mult)\
                           .then_inc(s_vs, 1)
                        dve.wait_ge(s_vs, 2)
                        L = 2 * Hh + 2
                        with dve.Fori(0, T // 2) as i:
                            for k in range(2):
                                t = i * 2 + k
                                st = Steps(dve, s_ch2, base=t * L)
                                for h in range(Hh):
                                    dve.wait_ge(s_t, t * Hh + (h + 2))
                                    prod = PR[h % 2]
                                    for c in range(3):
                                        last = dve.tensor_tensor(prod[:, c * JC:(c + 1) * JC, :],
                                                                 bank[2 + 3 * (h % 2) + c][:, 0:JC * D1].rearrange("p (j e) -> p j e", e=D1),
                                                                 spread(QA[:, t, h, c * JC:(c + 1) * JC], 2, D1), ALU.mult)
                                    st.then(last)
                                    dve.sem_inc(s_tf, 1)
                                    st.then(dve.tensor_reduce(Y[:, h, :], prod[:, :, :].rearrange("p j e -> p e j"), AX.X, ALU.add))
                                st.then(dve.tensor_tensor(Y[:, :, :], Y[:, :, :], vs[:, :, :], ALU.add))
                                st.then(dve.reciprocal(ry[:, :], Y[:, :, 0]))
                                assert st.n == L
                                dve.tensor_tensor(O[k][:, :, :], Y[:, :, 1:D1], spread(ry[:, :], 2, D), ALU.mult).then_inc(s_o, 1)
                                dve.wait_ge(s_pr, t + 1)
                                dve.tensor_tensor(X[:, t, :], X[:, t, :], bank[k][:, 0:C], ALU.add)


        def experts_stage():
            F = a["L0_ffn_W1s"].shape[1]
            NE = a["L0_ffn_W1p"].shape[0]
            FB = F // P
            NX = NE + 1
            tmp = ExitStack()
            s_c, s_stg, s_sf, s_lg, s_lc = sem("ex_const"), sem("ex_staged"), sem("ex_stage_free"), sem("ex_logits"), sem("ex_logits_copied")
            s_ch, s_e, s_d, s_mk, s_mt, s_mc = sem("ex_chain"), sem("ex_exp"), sem("ex_diff"), sem("ex_masks"), sem("ex_mask_turned"), sem("ex_mask_copied")
            s_w = [sem("ex_weights0"), sem("ex_weights1")]
            s_h, s_g, s_y, s_yf = sem("ex_hidden"), sem("ex_gelu"), sem("ex_out"), sem("ex_out_added")
            s_b, s_bt, s_b2 = sem("ex_bias_turned"), sem("ex_bias_copied"), sem("ex_bias2")
            with tmp:
                w1 = [sb(tmp, f"w1_{k}", [P, CB, F]) for k in range(2)]
                w2 = [sb(tmp, f"w2_{k}", [P, FB, C]) for k in range(2)]
                hid = sb(tmp, "hidden", [P, FB, W])
                b1r = sb(tmp, "b1_rows", [NX * FB, P])
                b1 = sb(tmp, "b1_cols", [P, NX * FB])
                b2 = sb(tmp, "b2_rows", [NX, C])
                wr = sb(tmp, "router", [P, CB, NE])
                stg = [sb(tmp, f"ex_cols{k}", [P, CB, P]) for k in range(2)]
                lg = sb(tmp, "logits", [P, T, NE])
                top8 = sb(tmp, "top8", [P, T, 8])
                ix = sb(tmp, "top8_index", [P, T, 8], mybir.dt.uint32)
                ixf = sb(tmp, "top8_float", [P, T, 8])
                d = sb(tmp, "top_weights", [P, 4, T])
                ioi = sb(tmp, "expert_ints", [P, NE], i32)
                iof = sb(tmp, "expert_floats", [P, NE])
                eq = [sb(tmp, f"chosen{k}", [P, T, NE]) for k in range(2)]
                mk = sb(tmp, "expert_weight", [P, T, NX])
                mkT = sb(tmp, "expert_weight_turned", [NX, NP])

                with nc.Block() as block:
                    @block.sync
                    def _(sp):
                        sp.dma_start(b1r[0:FB, :], a["L0_ffn_b1s"].rearrange("(f p) -> f p", p=P)).then_inc(s_c, 16)
                        sp.dma_start(b1r[FB:NX * FB, :], a["L0_ffn_b1p"].rearrange("e (f p) -> (e f) p", p=P)).then_inc(s_c, 16)
                        sp.dma_start(wr[:, :, :], a["L0_ffn_Wr"].rearrange("(k p) e -> p k e", p=P)).then_inc(s_c, 16)
                        sp.dma_start(b2[0:1, :], a["L0_ffn_b2s"].rearrange("(o c) -> o c", o=1)).then_inc(s_c, 16)
                        sp.dma_start(b2[1:NX, :], a["L0_ffn_b2p"]).then_inc(s_c, 16)
                        sp.dma_start(w1[0][:, :, :], a["L0_ffn_W1s"].rearrange("(k p) f -> p k f", p=P)).then_inc(s_w[0], 16)
                        sp.dma_start(w2[0][:, :, :], a["L0_ffn_W2s"].rearrange("(f p) c -> p f c", p=P)).then_inc(s_w[0], 16)
                        with sp.Fori(0, NE // 2) as i:
                            for r, k in enumerate((1, 0)):
                                m = i * 2 + (r + 1)
                                sp.wait_ge(s_y, (i * 2 + r) * T + 1)
                                sp.dma_start(w1[k][:, :, :], a["L0_ffn_W1p"][i * 2 + r].rearrange("(k p) f -> p k f", p=P)).then_inc(s_w[k], 16)
                                sp.dma_start(w2[k][:, :, :], a["L0_ffn_W2p"][i * 2 + r].rearrange("(f p) c -> p f c", p=P)).then_inc(s_w[k], 16)

                    @block.gpsimd
                    def _(pool):
                        pool.iota(ioi[:, :], [[1, NE]], base=0, channel_multiplier=0).then_inc(s_mk, 1)
                        pool.wait_ge(s_c, 80)
                        with pool.Fori(0, T // 2) as i:
                            for k in range(2):
                                t = i * 2 + k
                                if k == 0:
                                    pool.wait_ge(s_lg, i * 2 + 1)
                                pool.tensor_copy(stg[k][:, :, :], XT[:, :, ds(t * P, P)]).then_inc(s_stg, 1)

                    @block.tensor
                    def _(pe):
                        pe.wait_ge(s_c, 80)
                        pe.transpose(bank[7][:, 0:NX * FB], b1r[:, :], ident[0:NX * FB, 0:NX * FB]).then_inc(s_b, 1)
                        pe.sem_inc(s_lc, 2)
                        pe.sem_inc(s_lg, 1)
                        with pe.Fori(0, T // 2) as i:
                            for k in range(2):
                                t = i * 2 + k
                                pe.wait_ge(s_stg, t + 1)
                                pe.wait_ge(s_lc, t + 1)
                                for c in range(CB):
                                    last = pe.matmul(bank[k][:, 0:NE], stg[k][:, c, :], wr[:, c, :], start=c == 0, stop=c == CB - 1)
                                last.then_inc(s_lg, 1)

                        pe.sem_inc(s_yf, WT)
                        pe.sem_inc(s_y, 1)
                        pe.wait_ge(s_lc, T + 2)

                        def expert(m, buf, arrived):
                            with pe.Fori(0, NB) as b:
                                n = m * NB + b
                                pe.wait_ge(s_w[buf], arrived)
                                for f in range(FB):
                                    if f >= 2:
                                        pe.wait_ge(s_g, n * FB + (f - 1))
                                    for c in range(CB):
                                        last = pe.matmul(bank[f % 2][:, :], w1[buf][:, c, f * P:(f + 1) * P], XT[:, c, ds(b * W, W)],
                                                         start=c == 0, stop=c == CB - 1)
                                    last.then_inc(s_h, 1)
                                pe.wait_ge(s_g, n * FB + FB)
                                for j in range(WT):
                                    pe.wait_ge(s_yf, n * WT + (j + 1))
                                    for f in range(FB):
                                        last = pe.matmul(bank[2 + j][:, 0:C], hid[:, f, j * P:(j + 1) * P], w2[buf][:, f, :],
                                                         start=f == 0, stop=f == FB - 1)
                                    last.then_inc(s_y, 1)

                        expert(0, 0, 32)
                        pe.wait_ge(s_mk, 2)
                        for t in range(T):
                            if t % 4 == 0 and t:
                                pe.wait_ge(s_mc, t // 4)
                            last = pe.transpose(bank[6][0:NX, (t % 4) * P:(t % 4 + 1) * P], mk[:, t, :], ident[:, :])
                            if t % 4 == 3:
                                last.then_inc(s_mt, 1)
                        pe.wait_ge(s_mc, NB)
                        for t in range(T):
                            if t >= 2:
                                pe.wait_ge(s_b2, t - 1)
                            pe.matmul(bank[6 + t % 2][:, 0:C], mkT[:, t * P:(t + 1) * P], b2[:, :], start=True, stop=True).then_inc(s_mt, 1)
                        with pe.Fori(0, NE // 2) as i:
                            for r, k in enumerate((1, 0)):
                                expert(i * 2 + (r + 1), k, i * 32 + (32 if k == 1 else 64))

                    @block.scalar
                    def _(act):
                        act.wait_ge(s_b, 1)
                        act.activation(b1[:, :], bank[7][:, 0:NX * FB], ACT.Copy).then_inc(s_bt, 1)
                        act.wait_ge(s_d, 1)
                        act.activation(d[:, 1, :], d[:, 0, :], ACT.Exp).then_inc(s_e, 1)
                        act.wait_ge(s_bt, 1)

                        def expert(m):
                            with act.Fori(0, NB) as b:
                                n = m * NB + b
                                act.wait_ge(s_y, n * WT + 1)
                                for f in range(FB):
                                    act.wait_ge(s_h, n * FB + (f + 1))
                                    act.activation(hid[:, f, :], bank[f % 2][:, :], ACT.Gelu, bias=b1[:, ds(m * FB + f, 1)]).then_inc(s_g, 1)

                        expert(0)
                        for b in range(NB):
                            act.wait_ge(s_mt, b + 1)
                            act.activation(mkT[:, b * W:(b + 1) * W], bank[6][0:NX, :], ACT.Copy).then_inc(s_mc, 1)
                        with act.Fori(1, NX) as m:
                            expert(m)

                    @block.vector
                    def _(dve):
                        st = Steps(dve, s_ch)
                        dve.wait_ge(s_mk, 1)
                        st.then(dve.tensor_copy(iof[:, :], ioi[:, :]))
                        with dve.Fori(0, T // 2) as i:
                            for k in range(2):
                                t = i * 2 + k
                                dve.wait_ge(s_lg, t + 2)
                                dve.tensor_copy(lg[:, t, :], bank[k][:, 0:NE]).then_inc(s_lc, 1)
                        dve.wait_ge(s_lc, T + 2)
                        for t in range(T):
                            last = dve.max(top8[:, t, :], lg[:, t, :])
                        st.then(last)
                        for t in range(T):
                            last = dve.max_index(ix[:, t, :], top8[:, t, :], lg[:, t, :])
                        st.then(last)
                        dve.tensor_tensor(d[:, 0, :], top8[:, :, 1], top8[:, :, 0], ALU.subtract).then_inc(s_d, 1)
                        st.then(dve.tensor_copy(ixf[:, :, :], ix[:, :, :]))
                        dve.wait_ge(s_e, 1)
                        st.then(dve.tensor_scalar(d[:, 2, :], d[:, 1, :], 1.0, None, ALU.add))
                        st.then(dve.reciprocal(d[:, 2, :], d[:, 2, :]))
                        st.then(dve.tensor_tensor(d[:, 3, :], d[:, 1, :], d[:, 2, :], ALU.mult))
                        for k in range(2):
                            st.then(dve.tensor_tensor(eq[k][:, :, :], spread(iof[:, :], 1, T), spread(ixf[:, :, k], 2, NE), ALU.is_equal))
                            st.then(dve.tensor_tensor(eq[k][:, :, :], eq[k][:, :, :], spread(d[:, 2 + k, :], 2, NE), ALU.mult))
                        dve.memset(mk[:, :, 0:1], 1.0)
                        dve.tensor_tensor(mk[:, :, 1:NX], eq[0][:, :, :], eq[1][:, :, :], ALU.add).then_inc(s_mk, 1)
                        dve.wait_ge(s_mk, 2)

                        def expert(m):
                            with dve.Fori(0, NB) as b:
                                n = m * NB + b
                                dve.wait_ge(s_yf, m * T + WT)
                                for j in range(WT):
                                    dve.wait_ge(s_y, n * WT + (j + 2))
                                    dve.scalar_tensor_tensor(out=X[:, b * WT + j, :], in0=bank[2 + j][:, 0:C],
                                                             scalar=mk[:, b * WT + j, ds(m, 1)], in1=X[:, b * WT + j, :],
                                                             op0=ALU.mult, op1=ALU.add).then_inc(s_yf, 1)

                        expert(0)
                        dve.wait_ge(s_yf, WT + T)
                        for t in range(T):
                            dve.wait_ge(s_mt, NB + t + 1)
                            dve.tensor_tensor(X[:, t, :], X[:, t, :], bank[6 + t % 2][:, 0:C], ALU.add).then_inc(s_b2, 1)
                        dve.wait_ge(s_b2, T)
                        with dve.Fori(1, NX) as m:
                            expert(m)

        def linear_attention_stage(F):
            Hh = 8
            I = a["L1_mix_w_out"].shape[0]
            Dh = I // Hh
            IB = I // P
            tmp = ExitStack()
            s_w, s_c, s_stg, s_sf, s_kv = sem("la_weights"), sem("la_centred"), sem("la_staged"), sem("la_stage_free"), sem("la_kv")
            s_sq, s_ss, s_rt, s_ch, s_v = sem("la_square"), sem("la_sums"), sem("la_root"), sem("la_chain"), sem("la_v")
            s_k, s_use, s_z, s_dt, s_r, s_rc = sem("la_k"), sem("la_used"), sem("la_zero"), sem("la_dots"), sem("la_r"), sem("la_r_copied")
            with tmp:
                wc = sb(tmp, "w_kv", [P, CB, 2 * I])
                wm = sb(tmp, "w_kv_mean", [P, CB, 2 * Hh])
                wq = sb(tmp, "w_q", [P, IB, C])
                wo = sb(tmp, "w_o", [P, IB, C])
                stg = [sb(tmp, f"la_cols{k}", [P, CB, P]) for k in range(2)]
                sq = [sb(tmp, f"la_sq{k}", [P, 2 * I]) for k in range(2)]
                ss = [sb(tmp, f"la_ss{k}", [P, 3, 2 * Hh]) for k in range(2)]
                V = [sb(tmp, f"la_v{k}", [P, I]) for k in range(2)]
                K = [sb(tmp, f"la_k{k}", [P, I]) for k in range(2)]
                DT = sb(tmp, "dots", [P, IB, P])
                R = sb(tmp, "dots_out", [P, IB, C])
                zero = sb(tmp, "la_zero", [P, P])

                def by_head(ap):
                    return ap.rearrange("p (h d) -> p h d", d=Dh)

                with nc.Block() as block:
                    @block.sync
                    def _(sp):
                        sp.dma_start(wc[:, :, :], a["L1_mix_w_kv"].rearrange("(k p) o -> p k o", p=P)).then_inc(s_w, 16)
                        sp.dma_start(wq[:, :, :], a["L1_mix_w_qkv"][0:I, :].rearrange("(k p) c -> p k c", p=P)).then_inc(s_w, 16)
                        sp.dma_start(wo[:, :, :], a["L1_mix_w_out"].rearrange("(k p) c -> p k c", p=P)).then_inc(s_w, 16)

                    @block.gpsimd
                    def _(pool):
                        pool.memset(zero[:, :], 0.0).then_inc(s_z, 1)
                        pool.memset(DT[:, :, :], 0.0).then_inc(s_z, 1)
                        pool.sem_inc(s_sf, 2)
                        with pool.Fori(0, T // 2) as i:
                            for k in range(2):
                                t = i * 2 + k
                                pool.wait_ge(s_sf, t + 1)
                                pool.tensor_copy(stg[k][:, :, :], XT[:, :, ds(t * P, P)]).then_inc(s_stg, 1)

                    @block.tensor
                    def _(pe):
                        pe.wait_ge(s_c, 1)
                        pe.wait_ge(s_z, 2)
                        pe.matmul(bank[4][:, :], zero[:, :], wc[:, 0, 0:W], start=True, stop=False)

                        def kv(t, k):
                            pe.wait_ge(s_stg, t + 1)
                            pe.wait_ge(s_sf, t + 1)
                            for half in range(2):
                                for c in range(CB):
                                    last = pe.matmul(bank[2 * k + half][:, :], stg[k][:, c, :], wc[:, c, half * I:(half + 1) * I],
                                                     start=c == 0, stop=c == CB - 1)
                            last.then_inc(s_kv, 1)

                        def dots(t, k):
                            pe.wait_ge(s_k, t + 1)
                            pe.wait_ge(s_v, t + 1)
                            for p in range(IB):
                                last = pe.matmul(bank[4][:, p * P:(p + 1) * P], V[k][:, p * P:(p + 1) * P], K[k][:, p * P:(p + 1) * P],
                                                 start=False, stop=False, skip_group_check=True)
                            last.then_inc(s_use, 1)

                        kv(0, 0)
                        with pe.Fori(0, T // 2 - 1) as i:
                            for k in range(2):
                                kv(i * 2 + (k + 1), 1 - k)
                                dots(i * 2 + k, k)
                        kv(T - 1, 1)
                        dots(T - 2, 0)
                        dots(T - 1, 1)
                        pe.matmul(bank[4][:, :], zero[:, :], wc[:, 0, 0:W], start=False, stop=True).then_inc(s_dt, 1)
                        pe.wait_ge(s_dt, 2)
                        for p in range(IB):
                            last = pe.matmul(bank[p][:, 0:C], DT[:, p, :], wo[:, p, :], start=True, stop=True)
                        last.then_inc(s_r, 1)
                        pe.wait_ge(s_rc, 1)
                        for c in range(CB):
                            for p in range(IB):
                                last = pe.matmul(bank[5 + c][:, 0:C], wq[:, p, c * P:(c + 1) * P], R[:, p, :], start=p == 0, stop=p == IB - 1)
                        last.then_inc(s_r, 1)

                    @block.scalar
                    def _(act):
                        with act.Fori(0, T // 2) as i:
                            for k in range(2):
                                t = i * 2 + k
                                act.wait_ge(s_kv, t + 1)
                                for half in range(2):
                                    act.activation(sq[k][:, half * I:(half + 1) * I], bank[2 * k + half][:, :], ACT.Square).then_inc(s_sq, 1)
                                act.wait_ge(s_sf, t + 1)
                                act.activation(V[k][:, :], bank[2 * k + 1][:, :], ACT.Copy).then_inc(s_v, 1)
                                act.wait_ge(s_ss, t + 1)
                                act.activation(ss[k][:, 0, :], ss[k][:, 1, :], ACT.Sqrt).then_inc(s_rt, 1)

                    @block.vector
                    def _(dve):
                        st = Steps(dve, s_ch)
                        dve.wait_ge(s_w, 48)
                        for c in range(CB):
                            st.then(dve.tensor_reduce(wm[:, c, :], by_head(wc[:, c, :]), AX.X, ALU.add))
                        st.then(dve.tensor_scalar(wm[:, :, :], wm[:, :, :], 1.0 / Dh, None, ALU.mult))
                        for c in range(CB):
                            last = dve.tensor_tensor(by_head(wc[:, c, :]), by_head(wc[:, c, :]), spread(wm[:, c, :], 2, Dh), ALU.subtract)
                        last.then_inc(s_c, 1)
                        first = st.n
                        L = 7
                        with dve.Fori(0, T // 2) as i:
                            for k in range(2):
                                t = i * 2 + k
                                st = Steps(dve, s_ch, base=t * L + first)
                                dve.wait_ge(s_sq, t * 2 + 2)
                                st.then(dve.tensor_reduce(ss[k][:, 2, :], by_head(sq[k][:, :]), AX.X, ALU.add))
                                dve.tensor_scalar(ss[k][:, 1, :], ss[k][:, 2, :], 1.0 / Dh, 1e-5, ALU.mult, ALU.add).then_inc(s_ss, 1)
                                dve.wait_ge(s_rt, t + 1)
                                st.then(dve.reciprocal(ss[k][:, 0, :], ss[k][:, 0, :]))
                                newton_rsqrt(dve, st, ss[k][:, 0, :], ss[k][:, 1, :], ss[k][:, 2, :])
                                st.then(dve.tensor_tensor(ss[k][:, 2, 0:Hh], ss[k][:, 0, 0:Hh], ss[k][:, 0, Hh:2 * Hh], ALU.mult))
                                assert st.n == L
                                dve.wait_ge(s_v, t + 1)
                                dve.tensor_tensor(by_head(K[k][:, :]), by_head(bank[2 * k][:, :]), spread(ss[k][:, 2, 0:Hh], 2, Dh), ALU.mult)\
                                   .then_inc(s_k, 1)
                                dve.wait_ge(s_k, t + 1)
                                dve.sem_inc(s_sf, 1)
                        dve.wait_ge(s_dt, 1)
                        for p in range(IB):
                            for q in range(2):
                                r = slice(q * Dh, (q + 1) * Dh)
                                last = dve.tensor_scalar(DT[r, p, r], bank[4][r, p * P + q * Dh:p * P + (q + 1) * Dh], 1.0 / N, None, ALU.mult)
                        last.then_inc(s_dt, 1)
                        dve.wait_ge(s_r, 1)
                        for p in range(IB):
                            last = dve.tensor_copy(R[:, p, :], bank[p][:, 0:C])
                        last.then_inc(s_rc, 1)
                        dve.wait_ge(s_r, 2)
                        for c in range(CB):
                            dve.tensor_copy(F[:, c, :], bank[5 + c][:, 0:C])

        def slice_stage(R, WTT):
            Hh, G = 8, a["L1_ffn_W_slice"].shape[1]
            D = a["L1_ffn_W_slice"].shape[0]
            I = Hh * D
            IB = I // P
            tmp = ExitStack()
            s_w, s_z, s_ch, s_pre, s_fold, s_bf = sem("sl_weights"), sem("sl_zero"), sem("sl_chain"), sem("sl_pre"), sem("sl_folded"), sem("sl_fold_copied")
            s_stg, s_sf, s_lg, s_sub, s_exp = sem("sl_staged"), sem("sl_stage_free"), sem("sl_logits"), sem("sl_less_max"), sem("sl_exp")
            s_p, s_pt, s_pc, s_zt, s_x = sem("sl_weights_out"), sem("sl_turned"), sem("sl_turned_copied"), sem("sl_sums"), sem("sl_tail")
            s_y = sem("sl_tail_copied")
            with tmp:
                wx = sb(tmp, "w_x", [P, IB, C])
                wsl = sb(tmp, "w_slice", [P, 2 * G])
                wqkv = sb(tmp, "w_slice_qkv", [P, 3, P])
                wfx = sb(tmp, "w_fx", [P, CB, I])
                wo = sb(tmp, "w_out_sl", [P, IB, C])
                bx = sb(tmp, "b_x", [P, IB])
                bfx = sb(tmp, "b_fx", [P, IB])
                bsl = sb(tmp, "b_slice", [P, G])
                tm = sb(tmp, "sl_temp", [P, Hh])
                wf = sb(tmp, "w_folded", [P, CB, I])
                bf = sb(tmp, "b_folded", [P, I])
                bxr = sb(tmp, "b_x_wide", [P, IB, P])
                stg = [sb(tmp, f"sl_cols{k}", [P, CB, P]) for k in range(2)]
                lg = [sb(tmp, f"sl_lg{k}", [P, I]) for k in range(2)]
                mx = [sb(tmp, f"sl_mx{k}", [P, 2, Hh]) for k in range(2)]
                pr = [sb(tmp, f"sl_pr{k}", [P, I]) for k in range(2)]
                xs = [sb(tmp, f"sl_x{k}", [P, C]) for k in range(2)]
                ones = [sb(tmp, f"sl_ones{k}", [P, P]) for k in range(2)]
                ZT = sb(tmp, "sl_zt", [P, CB, I])
                nr = sb(tmp, "sl_norm", [P, 2, I])
                tok = sb(tmp, "sl_tok", [P, IB, P])
                qT = sb(tmp, "sl_qT", [P, IB, P])
                kT = sb(tmp, "sl_kT", [P, IB, P])
                vT = sb(tmp, "sl_vT", [P, IB, P])
                U = sb(tmp, "sl_u", [P, IB, C])
                at = sb(tmp, "sl_at", [P, IB, G])
                am = sb(tmp, "sl_am", [P, 2, IB])
                ab = sb(tmp, "sl_ab", [P, IB, P])
                abT = sb(tmp, "sl_abT", [P, IB, P])

                def by_head(ap):
                    return ap.rearrange("p (h g) -> p h g", g=G)

                with nc.Block() as block:
                    @block.sync
                    def _(sp):
                        sp.wait_ge(s_z, 1)
                        for q in range(2):
                            r = slice(q * D, (q + 1) * D)
                            sp.dma_start(wsl[r, q * G:(q + 1) * G], a["L1_ffn_W_slice"]).then_inc(s_w, 16)
                            for n, x in enumerate("qkv"):
                                sp.dma_start(wqkv[r, n, q * D:(q + 1) * D], a[f"L1_ffn_W_{x}"]).then_inc(s_w, 16)
                        sp.dma_start(wx[:, :, :], a["L1_ffn_W_x"].rearrange("(k p) c -> p k c", p=P)).then_inc(s_w, 16)
                        sp.dma_start(wfx[:, :, :], a["L1_ffn_W_fx"].rearrange("(k p) o -> p k o", p=P)).then_inc(s_w, 16)
                        sp.dma_start(wo[:, :, :], a["L1_ffn_W_out"].rearrange("(k p) c -> p k c", p=P)).then_inc(s_w, 16)
                        for k in range(IB):
                            sp.dma_start(bx[:, k:k + 1], a["L1_ffn_b_x"][k * P:(k + 1) * P].rearrange("(p o) -> p o", o=1)).then_inc(s_w, 16)
                            sp.dma_start(bfx[:, k:k + 1], a["L1_ffn_b_fx"][k * P:(k + 1) * P].rearrange("(p o) -> p o", o=1)).then_inc(s_w, 16)
                        sp.dma_start(bsl[:, :], rows(a["L1_ffn_b_slice"])).then_inc(s_w, 16)
                        sp.dma_start(tm[:, :], rows(a["L1_ffn_temperature"].rearrange("a h b c -> (a h b c)"))).then_inc(s_w, 16)
                    loads = 8 + 3 + 2 * IB + 2

                    @block.gpsimd
                    def _(pool):
                        pool.memset(wsl[:, :], 0.0)
                        pool.memset(tok[:, :, :], 0.0)
                        pool.memset(ab[:, :, :], 0.0)
                        pool.memset(wqkv[:, :, :], 0.0).then_inc(s_z, 1)
                        pool.sem_inc(s_sf, 1)
                        with pool.Fori(0, T // 2) as i:
                            for k in range(2):
                                t = i * 2 + k
                                pool.wait_ge(s_sf, t + 1)
                                pool.tensor_copy(xs[k][:, :], XN[:, t, :])
                                pool.tensor_copy(stg[k][:, :, :], XT[:, :, ds(t * P, P)]).then_inc(s_stg, 1)

                    @block.tensor
                    def _(pe):
                        pe.wait_ge(s_w, 16 * loads)
                        pe.wait_ge(s_pre, 1)
                        for c in range(CB):
                            for p in range(IB):
                                pe.matmul(bank[c][:, p * P:(p + 1) * P], wx[:, p, c * P:(c + 1) * P], wsl[:, :], start=True, stop=True)
                        for p in range(IB):
                            last = pe.matmul(bank[2][:, p * P:(p + 1) * P], bxr[:, p, :], wsl[:, :], start=True, stop=True)
                        last.then_inc(s_fold, 1)
                        pe.wait_ge(s_bf, 1)

                        def logits(t, k):
                            pe.wait_ge(s_stg, t + 1)
                            if not isinstance(t, int) or t > 0:
                                pe.wait_ge(s_sub, t)
                            for c in range(CB):
                                last = pe.matmul(bank[3][:, :], stg[k][:, c, :], wf[:, c, :], start=c == 0, stop=c == CB - 1)
                            last.then_inc(s_lg, 1)

                        def sums(t, k, first, final):
                            pe.wait_ge(s_p, t + 1)
                            pe.wait_ge(s_pc, t + 1)
                            for p in range(IB):
                                last = pe.transpose(bank[4][:, p * P:(p + 1) * P], pr[k][:, p * P:(p + 1) * P], ident[:, :])
                            last.then_inc(s_pt, 1)
                            for c in range(CB):
                                pe.matmul(bank[5 + c][:, :], xs[k][:, c * P:(c + 1) * P], pr[k][:, :], start=first, stop=final)
                            last = pe.matmul(bank[7][:, :], ones[1 if final else 0][:, :], pr[k][:, :], start=first, stop=final)
                            last.then_inc(s_zt, 1)

                        pe.sem_inc(s_pc, 1)
                        pe.sem_inc(s_zt, 1)
                        logits(0, 0)
                        logits(1, 1)
                        sums(0, 0, True, False)
                        with pe.Fori(0, T // 2 - 1) as i:
                            for k in range(2):
                                logits(i * 2 + (k + 2), k)
                                sums(i * 2 + (k + 1), 1 - k, False, False)
                        sums(T - 1, 1, False, True)
                        pe.wait_ge(s_pc, T + 1)
                        pe.wait_ge(s_x, 1)
                        for p in range(IB):
                            for c in range(CB):
                                last = pe.matmul(bank[0][:, p * P:(p + 1) * P], wfx[:, c, p * P:(p + 1) * P], ZT[:, c, p * P:(p + 1) * P],
                                                 start=c == 0, stop=c == CB - 1)
                        last.then_inc(s_y, 1)
                        pe.wait_ge(s_x, 2)
                        for n in range(3):
                            for p in range(IB):
                                last = pe.matmul(bank[1 + n][:, p * P:(p + 1) * P], wqkv[:, n, :], tok[:, p, :], start=True, stop=True)
                        last.then_inc(s_y, 1)
                        pe.wait_ge(s_x, 3)
                        for p in range(IB):
                            pe.matmul(bank[0][:, p * P:(p + 1) * P], qT[:, p, :], kT[:, p, :], start=True, stop=True)
                            last = pe.matmul(bank[4 + p][:, 0:C], vT[:, p, :], wo[:, p, :], start=True, stop=True)
                        last.then_inc(s_y, 1)
                        pe.wait_ge(s_x, 5)
                        for p in range(IB):
                            last = pe.transpose(bank[1][:, p * P:(p + 1) * P], ab[:, p, :], ident[:, :])
                        last.then_inc(s_y, 1)
                        pe.wait_ge(s_x, 6)
                        for p in range(IB):
                            last = pe.matmul(bank[4 + p][:, 0:C], abT[:, p, :], U[:, p, :], start=True, stop=True)
                        last.then_inc(s_y, 1)

                    @block.scalar
                    def _(act):
                        with act.Fori(0, T // 2) as i:
                            for k in range(2):
                                t = i * 2 + k
                                act.wait_ge(s_sub, t * 1 + 1)
                                act.wait_ge(s_exp, t * 2 + 1)
                                act.activation(pr[k][:, :], lg[k][:, :], ACT.Exp).then_inc(s_exp, 1)
                                act.wait_ge(s_pt, t + 1)
                                act.activation(WTT[:, :, ds(t * P, P)], bank[4][:, :].rearrange("p (q n) -> p q n", q=IB), ACT.Copy).then_inc(s_pc, 1)
                        act.wait_ge(s_x, 4)
                        act.activation(at[:, :, :], at[:, :, :], ACT.Exp).then_inc(s_bf, 1)

                    @block.vector
                    def _(dve):
                        st = Steps(dve, s_ch)
                        dve.wait_ge(s_w, 16 * loads)
                        for p in range(IB):
                            last = dve.tensor_scalar(bxr[:, p, :], onesf[:, :], bx[:, p:p + 1], None, ALU.mult)
                        last.then_inc(s_pre, 1)
                        dve.tensor_copy(ones[0][:, :], onesf[:, :])
                        st.then(dve.tensor_scalar(ones[1][:, :], onesf[:, :], mask[:, 0:1], None, ALU.mult))
                        st.then(dve.tensor_scalar(tm[:, :], tm[:, :], 0.1, 5.0, ALU.max, ALU.min))
                        st.then(dve.reciprocal(tm[:, :], tm[:, :]))
                        dve.wait_ge(s_fold, 1)
                        for c in range(CB):
                            dve.tensor_tensor(by_head(wf[:, c, :]), by_head(bank[c][:, :]), spread(tm[:, :], 2, G), ALU.mult)
                        st.then(dve.tensor_tensor(by_head(bf[:, :]), by_head(bank[2][:, :]), spread(bsl[:, :], 1, Hh), ALU.add))
                        dve.tensor_tensor(by_head(bf[:, :]), by_head(bf[:, :]), spread(tm[:, :], 2, G), ALU.mult).then_inc(s_bf, 1)
                        dve.wait_ge(s_bf, 1)
                        first = st.n
                        L = 3

                        def tile(t, k):
                            st = Steps(dve, s_ch, base=t * L + first)
                            dve.wait_ge(s_lg, t + 1)
                            dve.tensor_tensor(lg[k][:, :], bank[3][:, :], bf[:, :], ALU.add).then_inc(s_sub, 1)
                            dve.wait_ge(s_sub, t + 1)
                            st.then(dve.tensor_reduce(mx[k][:, 0, :], by_head(lg[k][:, :]), AX.X, ALU.max))
                            dve.tensor_tensor(by_head(lg[k][:, :]), by_head(lg[k][:, :]), spread(mx[k][:, 0, :], 2, G), ALU.subtract)\
                               .then_inc(s_exp, 1)
                            dve.wait_ge(s_exp, t * 2 + 2)
                            st.then(dve.tensor_reduce(mx[k][:, 1, :], by_head(pr[k][:, :]), AX.X, ALU.add))
                            st.then(dve.reciprocal(mx[k][:, 1, :], mx[k][:, 1, :]))
                            assert st.n == L
                            dve.tensor_tensor(by_head(pr[k][:, :]), by_head(pr[k][:, :]), spread(mx[k][:, 1, :], 2, G), ALU.mult)\
                               .then_inc(s_p, 1)

                        with dve.Fori(0, T // 2) as i:
                            for k in range(2):
                                t = i * 2 + k
                                tile(t, k)
                                dve.wait_ge(s_zt, t + 1)
                                dve.sem_inc(s_sf, 1)
                        st = Steps(dve, s_ch, base=first + T * L)
                        dve.wait_ge(s_zt, T + 1)
                        for c in range(CB):
                            last = dve.tensor_copy(ZT[:, c, :], bank[5 + c][:, :])
                        last.then_inc(s_x, 1)
                        dve.tensor_copy(nr[:, 0, :], bank[7][:, :])
                        st.then(dve.tensor_scalar(nr[:, 1, :], bank[7][:, :], 1e-5, None, ALU.add))
                        st.then(dve.reciprocal(nr[:, 1, :], nr[:, 1, :]))
                        dve.wait_ge(s_y, 1)
                        for p in range(IB):
                            for q in range(2):
                                r, c = slice(q * D, (q + 1) * D), slice(p * P + q * G, p * P + (q + 1) * G)
                                last = dve.scalar_tensor_tensor(out=tok[r, p, q * G:(q + 1) * G], in0=nr[r, 0, c], scalar=bfx[r, p:p + 1],
                                                                in1=bank[0][r, c], op0=ALU.mult, op1=ALU.add)
                        st.then(last)
                        for p in range(IB):
                            for q in range(2):
                                r, c = slice(q * D, (q + 1) * D), slice(p * P + q * G, p * P + (q + 1) * G)
                                last = dve.tensor_tensor(tok[r, p, q * G:(q + 1) * G], tok[r, p, q * G:(q + 1) * G], nr[r, 1, c], ALU.mult)
                        last.then_inc(s_x, 1)
                        dve.wait_ge(s_y, 2)
                        for n, x in enumerate((qT, kT, vT)):
                            last = dve.tensor_copy(x[:, :, :].rearrange("p b n -> p (b n)"), bank[1 + n][:, :])
                        last.then_inc(s_x, 1)
                        dve.wait_ge(s_y, 3)
                        for p in range(IB):
                            dve.tensor_copy(U[:, p, :], bank[4 + p][:, 0:C])
                            for q in range(2):
                                r = slice(q * G, (q + 1) * G)
                                last = dve.tensor_scalar(at[r, p, :], bank[0][r, p * P + q * G:p * P + (q + 1) * G], float(D) ** -0.5, None, ALU.mult)
                        st.then(last)
                        st.then(dve.tensor_reduce(am[:, 0, :], at[:, :, :], AX.X, ALU.max))
                        dve.tensor_tensor(at[:, :, :], at[:, :, :], spread(am[:, 0, :], 2, G), ALU.subtract).then_inc(s_x, 1)
                        dve.wait_ge(s_bf, 2)
                        st.then(dve.tensor_reduce(am[:, 1, :], at[:, :, :], AX.X, ALU.add))
                        st.then(dve.reciprocal(am[:, 1, :], am[:, 1, :]))
                        for p in range(IB):
                            for q in range(2):
                                r = slice(q * G, (q + 1) * G)
                                last = dve.tensor_scalar(ab[r, p, q * G:(q + 1) * G], at[r, p, :], am[r, 1, p:p + 1], None, ALU.mult)
                        last.then_inc(s_x, 1)
                        dve.wait_ge(s_y, 4)
                        dve.tensor_copy(abT[:, :, :].rearrange("p b n -> p (b n)"), bank[1][:, :]).then_inc(s_x, 1)
                        dve.wait_ge(s_y, 5)
                        for p in range(IB):
                            dve.tensor_copy(R[:, p, :], bank[4 + p][:, 0:C])

        xsplit = ExitStack()
        split = split_buffers(xsplit, "s0")
        rest = sb(xsplit, "rest0", [P, CB, NP])
        restv = rest[:, :, :].rearrange("p k n -> p (k n)").rearrange("p (t c) -> p t c", t=T)
        norm_stage("ln0", first=True, split=(*split, restv))
        if stages >= 1:
            edge_stage()
        if stages >= 2:
            sage_stage(split, rest)
        xsplit.close()
        if stages >= 3:
            taylor_stage()
        if stages >= 4:
            recycle()
            norm_stage("ln1")
            experts_stage()
        if stages >= 5:
            norm_stage("ln2")
            with ExitStack() as part:
                F = sb(part, "la_map", [P, CB, C])
                linear_attention_stage(F)
                project_stage("la_out", [(XT, [F[:, c, :] for c in range(CB)])], [], a["L1_mix_b_out"])
        if stages >= 6:
            with ExitStack() as part:
                split = split_buffers(part, "s1")
                mean = sb(part, "mean1", [P, CB, NP])
                rest = mean[:, :, :].rearrange("p k n -> p (k n)").rearrange("p (t c) -> p t c", t=T)
                recycle()
                norm_stage("ln2b", gamma=a["L1_gnn_gamma"], beta=a["L1_gnn_beta"], split=(*split, rest))
                with ExitStack() as inner:
                    sync, tensor, vector, _, _ = aggregate("agg1", inner, split, mean, None, None)
                    with nc.Block() as block:
                        block.sync(sync)
                        block.tensor(tensor)
                        block.vector(vector)
                wlr = sb(part, "sage1_w", [P, 2 * CB, C])
                project_stage("sage1", [(mean, [wlr[:, c, :] for c in range(CB)]), (XT, [wlr[:, CB + c, :] for c in range(CB)])],
                              [(wlr[:, n * CB:(n + 1) * CB, :], a[f"L1_gnn_W_{x}"].rearrange("(k p) o -> p k o", p=P)) for n, x in enumerate("lr")],
                              a["L1_gnn_b_l"])
        if stages >= 7:
            norm_stage("ln3")
            with ExitStack() as part:
                R = sb(part, "slice_out", [P, 4, C])
                WTT = sb(part, "slice_weights", [P, 4, NP])
                slice_stage(R, WTT)
                project_stage("last", [(WTT, [R[:, p, :] for p in range(4)])], [], a["L1_ffn_b_out"], out_dram=out)


TRANSPOSED = ["L0_gnn_W_l_f", "L0_gnn_W_r_f", "L0_gnn_W_l_b", "L0_gnn_W_r_b", "L0_mix_Wqkv", "L0_mix_Wproj",
              "L1_gnn_W_l", "L1_gnn_W_r", "L1_mix_w_out", "L1_ffn_W_x"]


def lay_out(inputs):
    import numpy as _np

    laid = {name: _np.asarray(value) for name, value in inputs.items()}
    laid.update({name: laid[name].T for name in TRANSPOSED})
    laid["L1_mix_w_kv"] = laid["L1_mix_w_qkv"][512:].T
    return laid


def kernel(**inputs):
    import numpy as _np
    import concourse.bacc as _bacc
    from concourse import mybir as _mybir
    from concourse.bass_utils import run_bass_kernel_spmd as _run

    nc = _bacc.Bacc("TRN2", target_bir_lowering=False, num_devices=1)
    arrays, args = {}, {}
    for name, value in lay_out(inputs).items():
        v = _np.asarray(value)
        arrays[f"in_{name}"] = _np.ascontiguousarray(v)
        args[name] = nc.dram_tensor(f"in_{name}", v.shape, _mybir.dt.from_np(v.dtype), kind="ExternalInput").ap()
    out = nc.dram_tensor("out_dram", args["x"].shape, _mybir.dt.float32, kind="ExternalOutput").ap()
    graph_network(nc, args, out)
    return _run(nc, [arrays], core_ids=[0]).results[0]["out_dram"]
```
